# Optimizing a Trainium2 kernel written in Bass

```python
import numpy as np
import jax
import jax.numpy as jnp

def _softmax(x, axis=-1):
    return jax.nn.softmax(x, axis=axis)

def _gelu(x):
    return jax.nn.gelu(x, approximate=True)

def _silu(x):
    return jax.nn.silu(x)

def _sigmoid(x):
    return jax.nn.sigmoid(x)

def _layernorm(x, axis=-1, eps=1e-05):
    m = jnp.mean(x, axis=axis, keepdims=True)
    v = jnp.var(x, axis=axis, keepdims=True)
    return (x - m) / jnp.sqrt(v + eps)

def _scatter_add(tgt, idx, src, axis=0):
    return tgt.at[idx].add(src)

def _segment_sum(src, seg, n):
    return jax.ops.segment_sum(src, seg, n)
kernel_name = 'mk_gnn_preln_d1_gnn_r64_02fad3'

def setup_inputs(seed: int=0):
    np.random.seed(seed)
    _w = jnp.asarray

    def _rec_inputs():
        import jax
        import jax.numpy as jnp
        _gk = jax.random.key(seed)
        x = -0.000929 + 1 * jax.random.normal(jax.random.fold_in(_gk, 1), (100000, 32), jnp.float32)
        src = jax.random.randint(jax.random.fold_in(_gk, 2), (25000,), 0, 100000, jnp.int32)
        dst = jax.random.randint(jax.random.fold_in(_gk, 3), (25000,), 0, 100000, jnp.int32)
        _o = jnp.argsort(dst, stable=True)
        src = src[_o]
        dst = dst[_o]
        edge_attr_4 = 0.00086875 + 0.999764 * jax.random.normal(jax.random.fold_in(_gk, 11), (25000, 4), jnp.float32)
        edge_attr_8 = jax.random.uniform(jax.random.fold_in(_gk, 12), (25000, 8), jnp.float32, 0.0, 1)
        return (x, src, dst, edge_attr_4, edge_attr_8)
    x, src, dst, edge_attr_4, edge_attr_8 = _rec_inputs()

    def _L0_gnn_setup():
        import jax, jax.numpy as jnp
        import numpy as np
        N = 512
        E = 8192
        MUL = 8
        NB = 8
        HR = 64
        NTP = 4 * MUL * MUL
        AVG_NEI = 16.0
        INV_SQRT3 = 1.0 / np.sqrt(3.0)
        ALPHA = 1.0 / np.sqrt(2.0 * MUL)
        key = jax.random.key(seed)
        ks = jax.random.split(key, 12)
        h = jax.random.normal(ks[0], (N, 4 * MUL), jnp.float32)
        edge_index = jax.random.randint(ks[1], (2, E), 0, N)
        edge_sh = jax.random.normal(ks[2], (E, 4), jnp.float32)
        edge_radial = jax.random.uniform(ks[3], (E, NB), jnp.float32)

        def lin(k, fi, fo):
            return (jax.random.normal(k, (fi, fo), jnp.float32) / np.sqrt(fi)).astype(jnp.float32)
        W1 = lin(ks[4], NB, HR)
        b1 = jnp.zeros((HR,), jnp.float32)
        W2 = lin(ks[5], HR, HR)
        b2 = jnp.zeros((HR,), jnp.float32)
        W3 = lin(ks[6], HR, NTP)
        b3 = jnp.zeros((NTP,), jnp.float32)
        Ws = jax.random.normal(ks[7], (MUL, MUL), jnp.float32)
        Wv = jax.random.normal(ks[8], (MUL, MUL), jnp.float32)
        return dict(h=h, edge_index=edge_index, edge_sh=edge_sh, edge_radial=edge_radial, n_atoms=N, W1=W1, b1=b1, W2=W2, b2=b2, W3=W3, b3=b3, Ws=Ws, Wv=Wv)
    _L0_gnn_all = _L0_gnn_setup()
    _L0_gnn_in = {k: v for k, v in _L0_gnn_all.items() if k in ('W1', 'b1', 'W2', 'b2', 'W3', 'b3', 'Ws', 'Wv')}
    del _L0_gnn_all
    return {'x': x, 'src': src, 'dst': dst, 'edge_attr_4': edge_attr_4, 'edge_attr_8': edge_attr_8, 'L0_gnn_W1': _L0_gnn_in['W1'], 'L0_gnn_b1': _L0_gnn_in['b1'], 'L0_gnn_W2': _L0_gnn_in['W2'], 'L0_gnn_b2': _L0_gnn_in['b2'], 'L0_gnn_W3': _L0_gnn_in['W3'], 'L0_gnn_b3': _L0_gnn_in['b3'], 'L0_gnn_Ws': _L0_gnn_in['Ws'], 'L0_gnn_Wv': _L0_gnn_in['Wv']}

def reference(x, src, dst, edge_attr_4, edge_attr_8, L0_gnn_W1, L0_gnn_b1, L0_gnn_W2, L0_gnn_b2, L0_gnn_W3, L0_gnn_b3, L0_gnn_Ws, L0_gnn_Wv):
    import jax
    import jax.numpy as jnp

    def _L0_gnn_ref(h, edge_index, edge_sh, edge_radial, n_atoms, W1, b1, W2, b2, W3, b3, Ws, Wv):
        import jax, jax.numpy as jnp
        import numpy as np
        N = 512
        E = 8192
        MUL = 8
        NB = 8
        HR = 64
        NTP = 4 * MUL * MUL
        AVG_NEI = 16.0
        INV_SQRT3 = 1.0 / np.sqrt(3.0)
        ALPHA = 1.0 / np.sqrt(2.0 * MUL)
        src, dst = (edge_index[0], edge_index[1])
        x = jax.nn.silu(edge_radial @ W1 + b1)
        x = jax.nn.silu(x @ W2 + b2)
        tpw = x @ W3 + b3
        P = MUL * MUL
        W00 = tpw[:, 0 * P:1 * P].reshape(-1, MUL, MUL)
        W110 = tpw[:, 1 * P:2 * P].reshape(-1, MUL, MUL)
        W01 = tpw[:, 2 * P:3 * P].reshape(-1, MUL, MUL)
        W10 = tpw[:, 3 * P:4 * P].reshape(-1, MUL, MUL)
        hs = h[:, :MUL]
        hv = h[:, MUL:].reshape(-1, MUL, 3)
        hs_e = hs[src]
        hv_e = hv[src]
        sh0 = edge_sh[:, 0]
        sh1 = edge_sh[:, 1:4]
        m0 = ALPHA * (jnp.einsum('eu,euw->ew', hs_e * sh0[:, None], W00) + INV_SQRT3 * jnp.einsum('eui,ei,euw->ew', hv_e, sh1, W110))
        m1 = ALPHA * (jnp.einsum('eu,ei,euw->ewi', hs_e, sh1, W01) + jnp.einsum('eui,euw->ewi', hv_e * sh0[:, None, None], W10))
        messages = jnp.concatenate([m0, m1.reshape(-1, 3 * MUL)], axis=-1)
        agg = jax.ops.segment_sum(messages, dst, num_segments=n_atoms) / np.sqrt(AVG_NEI)
        self0 = hs @ Ws / np.sqrt(MUL)
        self1 = jnp.einsum('nui,uw->nwi', hv, Wv) / np.sqrt(MUL)
        h_self = jnp.concatenate([self0, self1.reshape(-1, 3 * MUL)], axis=-1)
        return h_self + agg
    edge_index = jnp.stack([src, dst])
    h = jnp.maximum(_layernorm(x, axis=-1), 0.0)
    x = x + _L0_gnn_ref(h, edge_index, edge_attr_4, edge_attr_8, 100000, L0_gnn_W1, L0_gnn_b1, L0_gnn_W2, L0_gnn_b2, L0_gnn_W3, L0_gnn_b3, L0_gnn_Ws, L0_gnn_Wv)
    return x

_drawn_inputs = setup_inputs


def setup_inputs(seed=0):
    import zlib

    import numpy as np

    out = dict(_drawn_inputs(seed))
    spreads = {'L0_gnn_b1': (0.0, 0.8), 'L0_gnn_b2': (0.0, 2.0), 'L0_gnn_b3': (0.0, 2.0)}
    factors = {'edge_attr_4': 3.787,
     'edge_attr_8': 8.0,
     'L0_gnn_W1': 4.731,
     'L0_gnn_W2': 4.337,
     'L0_gnn_W3': 3.972,
     'L0_gnn_Ws': 8.0,
     'L0_gnn_Wv': 6.018}
    for name, (base, spread) in spreads.items():
        noise = np.random.default_rng([zlib.crc32(name.encode()), seed]).standard_normal(out[name].shape)
        drawn = base * np.exp(spread * noise) if base else spread * noise
        out[name] = jnp.asarray(drawn.astype(out[name].dtype))
    for name, factor in factors.items():
        out[name] = (out[name] * factor).astype(out[name].dtype)
    return out
```

```python
import numpy as np
import concourse.bass as bass
from concourse import mybir
from contextlib import ExitStack


def gnn_layer(nc, x, src, dst, edge_sh, edge_radial, W1, b1, W2, b2, W3, b3, Ws, Wv, out):
    f32, bf16, i32 = mybir.dt.float32, mybir.dt.bfloat16, mybir.dt.int32
    ALU = mybir.AluOpType
    ACT = mybir.ActivationFunctionType
    X = mybir.AxisListType.X
    ds = bass.ds

    P = 128
    N, D = x.shape
    E = src.shape[0]
    MUL = Ws.shape[0]
    NB, HR = W1.shape
    NTP = W3.shape[1]
    EPS = 1e-5
    SCALE = float(1.0 / np.sqrt(2.0 * MUL) / np.sqrt(16.0))
    INV_SQRT3 = float(1.0 / np.sqrt(3.0))
    SELF = float(1.0 / np.sqrt(MUL))

    R = 16
    FULL = N // (P * R)
    CH = [(c * P * R, P, R) for c in range(FULL)]
    rest = N - FULL * P * R
    R2 = rest // P // 4 * 4
    CH.append((FULL * P * R, P, R2))
    P3 = (rest - R2 * P) // 4
    CH.append((FULL * P * R + R2 * P, P3, 4))
    NCH = len(CH)
    XS = 4
    DBODY = 8
    DLOOP = FULL // DBODY

    T = E // P
    TAIL = E - T * P
    UT, BT = 8, 4
    NU = T // UT
    NQ = 2 * NU + 1
    assert T + 1 == NU * UT + BT and TAIL > 0
    EARLY = NU // 2
    assert EARLY * 4 == FULL
    SOFF = [0, 512, 896, 1152, 1280]
    NS = 4

    x_v = x
    er_main = edge_radial[0:T * P, :].rearrange("(p t) k -> p (t k)", p=P)
    sh_main = edge_sh[0:T * P, :].rearrange("(p t) k -> p (t k)", p=P)
    dst_main = dst[0:T * P].rearrange("(p t) -> p t", p=P)
    src_main = src[0:T * P].rearrange("(p t) -> p t", p=P)

    ctx = ExitStack()
    with ctx:
        def sb(name, shape, dt=f32):
            return ctx.enter_context(nc.sbuf_tensor(name, shape, dt))

        def sem(name):
            return ctx.enter_context(nc.semaphore(name))

        ident = sb("ident", [P, P])
        center = sb("center", [P, P])
        ones_g = sb("ones_g", [P, 4])
        wself = sb("wself", [P, P])
        wself32 = sb("wself32", [D, D])
        w1big = sb("w1big", [P, 4, P])
        w2blk = sb("w2blk", [P, P])
        w3blk = sb("w3blk", [P, 2 * NTP])
        b1col = sb("b1col", [P, 1])
        b2col = sb("b2col", [P, 1])
        epscol = sb("epscol", [P, 1])
        b3f = sb("b3f", [1, 2 * NTP])
        b3r = sb("b3r", [1, 2 * NTP])
        b3mid = sb("b3mid", [1, 2 * NTP], bf16)
        b3lo = sb("b3lo", [1, 2 * NTP], bf16)
        b3rows = sb("b3rows", [P, 2 * NTP], bf16)
        ones3 = sb("ones3", [P, P], bf16)
        later = sb("later", [P, BT * P])
        trash_i = sb("trash_i", [P, BT], i32)
        trash = sb("trash", [P, BT])
        spare0 = sb("spare0", [P, D * 4])
        xin = sb("xin", [P, XS, R * D])
        oc = sb("oc", [P, XS, R * D])
        xTs = sb("xTs", [P, 2, R * D])
        rT = sb("rT", [P, 2, R * D])
        sqT = sb("sqT", [P, 2, R * D])
        nstd = sb("nstd", [P, 2, R])
        nrstd = sb("nrstd", [P, 2, R])
        src_slot = [sb(f"src_slot{i}", [P, UT], i32) for i in range(3)]
        xg = [sb(f"xg{i}", [P, UT * D]) for i in range(3)]
        gsum = sb("gsum", [P, UT])
        gc = sb("gc", [P, UT * D])
        gsq = sb("gsq", [P, UT * D])
        gvar = sb("gvar", [P, UT])
        gstd = sb("gstd", [P, UT])
        grstd = sb("grstd", [P, UT])
        h_all = sb("h_all", [P, (T + 1) * D])
        sh_all = sb("sh_all", [P, (T + 1) * 4])
        dst_i = sb("dst_i", [P, T + 1], i32)
        dst_f = sb("dst_f", [P, T + 1])
        er = [sb(f"er{i}", [P, P]) for i in range(3)]
        erT = sb("erT", [P, P])
        x1 = sb("x1", [P, 4 * P])
        x2 = sb("x2", [P, 2, 4 * P])
        coef = sb("coef", [P, 2, UT, 6 * MUL])
        dotp = sb("dotp", [P, UT * 3 * MUL])
        prod = sb("prod", [P, BT, 6 * 64])
        red = sb("red", [P, BT, 6, MUL])
        outer = sb("outer", [P, BT, 3 * MUL])
        msg = sb("msg", [P, 2, BT, D])
        dcol = sb("dcol", [P, 2, BT])
        eq = sb("eq", [P, 2, SOFF[4]])
        cnt = sb("cnt", [P, BT])
        win = sb("win", [P, BT])
        dmt = sb("dmt", [P, BT])
        idx_f = sb("idx_f", [P, BT])
        idx_i = sb("idx_i", [P, NS, BT], i32)
        sums = sb("sums", [P, NS, BT * D])

        ps = ctx.enter_context(nc.psum_tensor("ps", [P, 8 * 512], f32))

        def bank(b, n=1):
            return ps[:, b * 512:(b + n) * 512]

        psXT = [bank(0), bank(1)]
        psXC = [bank(2), bank(3)]
        psY = [bank(4), bank(5)]
        psV = [bank(6)[:, 0:R], bank(7)[:, 0:R]]
        psTP = [bank(0, 2), bank(2, 2)]
        psMLP = bank(4)
        psER = bank(5)[:, 0:P]
        psDT = bank(6)
        psSUM = bank(7)[:, 0:BT * D]

        names = """zeroed w_loaded selfw_loaded selfw_scaled selfw_placed pool_const dve_const b3_split b3_placed
            spare_stored dst_pad dst_loaded dst_cast sh_loaded
            xT_ready xT_copied xc_ready rs_done v_ready y_ready std_done rstd_done y_used o_done
            gsum_done gc_done gsq_done gvar_done gstd_done grstd_done h_done
            erT_ready erT_copied l1_ready x1_done l2_ready x2_done
            dot_done coef_done tp_ready prod_done red_done outer_done msg_done
            dcol_done dT_ready eq_done win_done dmt_done idxf_done idx_done
            sum_ready sums_done scattered erlast_loaded dve_zero b3_scaled""".split()
        s = {n: sem(n) for n in names}
        x_loaded = [sem(f"x_loaded{i}") for i in range(XS)]
        stored = [sem(f"stored{i}") for i in range(XS)]
        src_loaded = [sem(f"src_loaded{i}") for i in range(3)]
        gathered = [sem(f"gathered{i}") for i in range(3)]
        er_loaded = [sem(f"er_loaded{i}") for i in range(2)]

        def rows(ap, c, base):
            _, p, r = CH[min(base, NCH - 1)]
            r0 = c * (P * R) if base < FULL else CH[base][0]
            return ap[ds(r0, p * r), :].rearrange("(p r) d -> p (r d)", p=p), p, r * D

        block = ctx.enter_context(nc.Block())

        @block.sync
        def _(sp):
            def load_src(u, slot):
                sp.dma_start(src_slot[slot][:, :], src_main[:, ds(u * UT, UT)]).then_inc(src_loaded[slot], 16)

            def load_er(u, slot):
                sp.dma_start(er[slot][:, 0:UT * NB], er_main[:, ds(u * UT * NB, UT * NB)])\
                  .then_inc(er_loaded[slot], 16)

            def load_x(c, base):
                if base >= XS:
                    sp.wait_ge(s["o_done"], c - XS + 1)
                v, p, n = rows(x_v, c, base)
                sp.dma_start(xin[0:p, base % XS, 0:n], v).then_inc(x_loaded[base % XS], 16)

            def store(c, base):
                sp.wait_ge(s["o_done"], c + 1)
                v, p, n = rows(out, c, base)
                sp.dma_start(v, oc[0:p, base % XS, 0:n]).then_inc(stored[base % XS], 16)

            load_src(0, 0)
            load_src(1, 1)
            load_x(0, 0)
            load_x(1, 1)
            sp.wait_ge(s["zeroed"], 1)
            sp.dma_start(wself32[0:MUL, 0:MUL], Ws).then_inc(s["selfw_loaded"], 16)
            for i in range(3):
                with nc.allow_non_contiguous_dma(reason="64 weights"):
                    sp.dma_start(wself32[MUL + i:D:3, MUL + i:D:3], Wv).then_inc(s["selfw_loaded"], 16)
            sp.dma_start(b3f[:, 0:NTP], b3.rearrange("(a n) -> a n", a=1)).then_inc(s["w_loaded"], 16)
            sp.dma_start(b3f[:, NTP:2 * NTP], b3.rearrange("(a n) -> a n", a=1)).then_inc(s["w_loaded"], 16)
            for h in range(2):
                sp.dma_start(w3blk[h * HR:(h + 1) * HR, h * NTP:(h + 1) * NTP], W3).then_inc(s["w_loaded"], 16)
                sp.dma_start(w2blk[h * HR:(h + 1) * HR, h * HR:(h + 1) * HR], W2).then_inc(s["w_loaded"], 16)
                sp.dma_start(b1col[h * HR:(h + 1) * HR, :], b1.rearrange("(n a) -> n a", a=1)).then_inc(s["w_loaded"], 16)
                sp.dma_start(b2col[h * HR:(h + 1) * HR, :], b2.rearrange("(n a) -> n a", a=1)).then_inc(s["w_loaded"], 16)
            for t in range(UT):
                sp.dma_start(w1big[t * NB:(t + 1) * NB, t // 2, (t % 2) * HR:(t % 2 + 1) * HR], W1)\
                  .then_inc(s["w_loaded"], 16)
            sp.wait_ge(s["selfw_scaled"], 1)
            for g in range(4):
                sp.dma_start(wself[g * D:(g + 1) * D, g * D:(g + 1) * D], wself32[:, :]).then_inc(s["selfw_placed"], 16)
            load_x(2, 2)
            load_x(3, 3)
            sp.dma_start(dst_i[:, 0:T], dst_main).then_inc(s["dst_loaded"], 16)
            sp.wait_ge(s["dst_pad"], 1)
            sp.dma_start(dst_i[0:TAIL, T:T + 1], dst[T * P:E].rearrange("(n a) -> n a", a=1)).then_inc(s["dst_loaded"], 16)
            sp.dma_start(sh_all[:, 0:T * 4], sh_main).then_inc(s["sh_loaded"], 16)
            sp.dma_start(sh_all[0:TAIL, T * 4:T * 4 + 4], edge_sh[T * P:E, :]).then_inc(s["sh_loaded"], 16)
            load_er(0, 0)
            load_er(1, 1)
            lt = T - NU * UT
            sp.dma_start(er[2][:, 0:lt * NB], er_main[:, NU * UT * NB:T * NB]).then_inc(s["erlast_loaded"], 16)
            sp.dma_start(er[2][0:TAIL, lt * NB:(lt + 1) * NB], edge_radial[T * P:E, :]).then_inc(s["erlast_loaded"], 16)
            sp.wait_ge(s["b3_split"], 1)
            sp.dma_start(b3rows[1:2, :], b3mid[:, :]).then_inc(s["b3_placed"], 16)
            sp.dma_start(b3rows[2:3, :], b3lo[:, :]).then_inc(s["b3_placed"], 16)
            sp.dma_start(out[N:N + BT * P, :].rearrange("(p r) d -> p (r d)", p=P), spare0[:, :]).then_inc(s["spare_stored"], 16)
            load_src(EARLY, 2)

            def node_pass(i, first):
                for k in range(DBODY):
                    c = i * DBODY + k
                    base = k if first else k + DBODY
                    if base >= XS:
                        store(c - XS, base - XS)
                        load_x(c, base)
                    if k in (3, 7):
                        slot = k // 4
                        sp.wait_ge(gathered[slot], (i + 1) * 16 * UT)
                        load_src(2 * i + 2 + slot, slot)

            node_pass(0, True)
            with sp.Fori(1, DLOOP - 1) as i:
                node_pass(i, False)
            for k in range(DBODY):
                c = (DLOOP - 1) * DBODY + k
                store(c - XS, c - XS)
                load_x(c, c)
            for c in range(FULL, NCH):
                store(c - XS, c - XS)
                load_x(c, c)
            for c in range(NCH - XS, NCH):
                store(c, c)

            def edge_pass(v):
                sp.wait_ge(gathered[2], (v + 1) * 16 * UT)
                load_src(EARLY + 1 + v, 2)
                for h in range(2):
                    sp.wait_ge(s["erT_ready"], 2 * v + h + 1)
                    load_er(2 * v + 2 + h, h)

            with sp.Fori(0, NU // 2 - 1) as v:
                edge_pass(v)
            v = NU // 2 - 1
            sp.wait_ge(gathered[2], (v + 1) * 16 * UT)
            sp.dma_start(src_slot[2][:, 0:lt], src_main[:, NU * UT:T]).then_inc(src_loaded[2], 16)
            sp.dma_start(src_slot[2][0:TAIL, lt:lt + 1], src[T * P:E].rearrange("(n a) -> n a", a=1)).then_inc(src_loaded[2], 16)

        @block.gpsimd
        def _(pool):
            pool.memset(ident[:, :], 0.0).then_inc(s["pool_const"], 1)
            pool.wait_ge(s["pool_const"], 1)
            pool.affine_select(out=ident[:, :], in_=ident[:, :], compare_op=ALU.not_equal, fill=1.0, base=0,
                               pattern=[[-1, P]], channel_multiplier=1).then_inc(s["pool_const"], 1)

            def gather(t, slot):
                pool.indirect_dma_start(xg[slot][:, t * D:(t + 1) * D], None, x,
                                        bass.IndirectOffsetOnAxis(ap=src_slot[slot][:, t:t + 1], axis=0))\
                    .then_inc(gathered[slot], 16)

            def gather_early(i, first):
                for slot in range(2):
                    pool.wait_ge(src_loaded[slot], 16 * (i + 1))
                    if not first:
                        pool.wait_ge(s["gc_done"], 2 * i + slot - 1)
                        pool.nop(nofuse=True)
                    for t in range(UT):
                        gather(t, slot)

            gather_early(0, True)
            pool.memset(later[:, :], 1.0).then_inc(s["pool_const"], 1)
            pool.wait_ge(s["pool_const"], 3)
            pool.affine_select(out=later[:, 0:P], in_=later[:, 0:P], compare_op=ALU.is_ge, fill=0.0, base=0,
                               pattern=[[1, P]], channel_multiplier=-1).then_inc(s["pool_const"], 1)
            pool.iota(trash_i[:, :], pattern=[[P, BT]], base=N, channel_multiplier=1).then_inc(s["pool_const"], 1)
            pool.iota(dst_i[:, T:T + 1], pattern=[[1, 1]], base=N + (BT - 1) * P, channel_multiplier=1)\
                .then_inc(s["dst_pad"], 1)
            with pool.Fori(1, EARLY // 2) as i:
                gather_early(i, False)
            pool.wait_ge(src_loaded[2], 16)
            for t in range(UT):
                gather(t, 2)

            def scatter(q, k):
                pool.wait_ge(s["sums_done"], q + 1)
                pool.wait_ge(s["idx_done"], q + 1)
                if k != 0:
                    pool.wait_ge(s["scattered"], q * 16 * BT)
                pool.nop(nofuse=True)
                for a in range(BT):
                    pool.indirect_dma_start(out, bass.IndirectOffsetOnAxis(ap=idx_i[:, k % NS, a:a + 1], axis=0),
                                            sums[:, k % NS, a * D:(a + 1) * D], None, compute_op=ALU.add)\
                        .then_inc(s["scattered"], 16)

            def edge_pass(v, first, last):
                for k in range(4):
                    if k == 0:
                        pool.wait_ge(src_loaded[2], 16 * (v + 2) + (16 if last else 0))
                        pool.wait_ge(s["gc_done"], EARLY + v + 1)
                        pool.nop(nofuse=True)
                    if not last or k < 2:
                        gather(2 * k, 2)
                        gather(2 * k + 1, 2)
                    scatter(4 * v + k, k if first else k + 4)

            for k in range(XS):
                pool.wait_ge(stored[k], 16 * len(range(k, NCH, XS)))
            pool.wait_ge(s["spare_stored"], 16)
            edge_pass(0, True, False)
            with pool.Fori(1, NU // 2 - 1) as v:
                edge_pass(v, False, False)
            edge_pass(NU // 2 - 1, False, True)
            scatter(NQ - 1, NQ - 1)
            pool.wait_ge(s["scattered"], NQ * 16 * BT)

        @block.scalar
        def _(act):
            def copy_xT(c, base):
                _, p, r = CH[base]
                n = r // 4 * P if base >= FULL else R * D
                act.wait_ge(s["xT_ready"], c + 1)
                if base >= 2:
                    act.wait_ge(s["xc_ready"], c - 1)
                act.activation(xTs[:, base % 2, 0:n], psXT[base % 2][:, 0:n], ACT.Copy).then_inc(s["xT_copied"], 1)

            def relu_square(c, base):
                _, p, r = CH[base]
                n = r // 4 * P if base >= FULL else R * D
                act.wait_ge(s["xc_ready"], c + 1)
                if base >= 2:
                    act.wait_ge(s["y_ready"], c - 1)
                act.activation(sqT[:, base % 2, 0:n], psXC[base % 2][:, 0:n], ACT.Square)
                act.activation(rT[:, base % 2, 0:n], psXC[base % 2][:, 0:n], ACT.Relu).then_inc(s["rs_done"], 1)

            def node_std(c, base):
                _, p, r = CH[base]
                act.wait_ge(s["v_ready"], c + 1)
                if base >= 2:
                    act.wait_ge(s["rstd_done"], c - 1)
                act.activation(nstd[0:p, base % 2, 0:r], psV[base % 2][0:p, 0:r], ACT.Sqrt,
                               bias=epscol[0:p, :]).then_inc(s["std_done"], 1)

            def feat_square(n, w=UT * D):
                act.wait_ge(s["gc_done"], n + 1)
                act.activation(gsq[:, 0:w], gc[:, 0:w], ACT.Square).then_inc(s["gsq_done"], 1)

            def feat_std(n, w=UT):
                act.wait_ge(s["gvar_done"], n + 1)
                act.activation(gstd[:, 0:w], gvar[:, 0:w], ACT.Sqrt, bias=epscol[:, :], scale=1.0 / D)\
                   .then_inc(s["gstd_done"], 1)

            act.wait_ge(s["dve_const"], 1)

            def node_step(c, base, i, feats=True):
                if base < NCH:
                    copy_xT(c, base)
                if 1 <= base <= NCH:
                    relu_square(c - 1, base - 1)
                if 2 <= base <= NCH + 1:
                    node_std(c - 2, base - 2)
                if feats and base % 4 == 1:
                    feat_square(2 * i + base % 8 // 4)
                if feats and base % 4 == 3:
                    feat_std(2 * i + base % 8 // 4)

            for k in range(DBODY):
                node_step(k, k, 0)
            with act.Fori(1, DLOOP) as i:
                for k in range(DBODY):
                    node_step(i * DBODY + k, k + DBODY, i)
            for c in range(FULL, NCH + 2):
                node_step(c, c, 0, False)

            def mlp_in(u, k):
                act.wait_ge(s["erT_ready"], u + 1)
                if k > 0:
                    act.wait_ge(s["l1_ready"], u)
                act.activation(erT[:, :], psER, ACT.Copy).then_inc(s["erT_copied"], 1)

            def mlp_one(u, k, w=4 * P):
                act.wait_ge(s["l1_ready"], u + 1)
                if k > 0:
                    act.wait_ge(s["l2_ready"], u)
                act.activation(x1[:, 0:w], psMLP[:, 0:w], ACT.Silu, bias=b1col[:, :]).then_inc(s["x1_done"], 1)

            def mlp_two(u, k, w=4 * P):
                act.wait_ge(s["l2_ready"], u + 1)
                if k > 1:
                    act.wait_ge(s["tp_ready"], 2 * u - 2)
                act.activation(x2[:, k % 2, 0:w], psMLP[:, 0:w], ACT.Silu, bias=b2col[:, :]).then_inc(s["x2_done"], 1)

            def copy_sums(q, k):
                act.wait_ge(s["sum_ready"], q + 1)
                if k >= NS:
                    act.wait_ge(s["scattered"], (q - NS + (2 if k % NS == NS - 1 else 1)) * 16 * BT)
                act.activation(sums[:, k % NS, :], psSUM, ACT.Copy).then_inc(s["sums_done"], 1)

            act.wait_ge(s["w_loaded"], 16 * (2 + 8 + UT))
            mlp_in(0, 0)
            mlp_one(0, 0)
            mlp_two(0, 0)

            def edge_pass(v, first, last):
                n = EARLY + v
                feat_square(n)
                feat_std(n)
                for h in range(2):
                    u, k = 2 * v + h, (h if first else h + 4)
                    w = 2 * P if last and h == 1 else 4 * P
                    mlp_in(u + 1, k + 1)
                    if not (first and h == 0):
                        copy_sums(2 * u - 1, 2 * k - 1)
                    mlp_one(u + 1, k + 1, w)
                    copy_sums(2 * u, 2 * k)
                    mlp_two(u + 1, k + 1, w)

            edge_pass(0, True, False)
            with act.Fori(1, NU // 2 - 1) as v:
                edge_pass(v, False, False)
            edge_pass(NU // 2 - 1, False, True)
            feat_square(NU, BT * D)
            feat_std(NU, BT)
            copy_sums(NQ - 2, NQ - 2)
            copy_sums(NQ - 1, NQ - 1)

        @block.tensor
        def _(pe):
            def transposes(c, base):
                _, p, r = CH[base]
                pe.wait_ge(x_loaded[base % XS], 16 * ((c - base % XS) // XS + 1) if isinstance(c, int)
                           else loaded_count(c, base))
                if base >= 2:
                    pe.wait_ge(s["xT_copied"], c - 1)
                for g in range(r // 4):
                    m = pe.transpose(psXT[base % 2][:, g * P:g * P + p], xin[0:p, base % XS, g * P:(g + 1) * P],
                                     ident[0:p, 0:p])
                m.then_inc(s["xT_ready"], 1)

            loaded = {}

            def loaded_count(c, base):
                return loaded["i"] * (16 * DBODY // XS) + 16 * ((base - DBODY) // XS + 1)

            def centre(c, base):
                _, p, r = CH[base]
                pe.wait_ge(s["xT_copied"], c + 1)
                if base >= 2:
                    pe.wait_ge(s["rs_done"], c - 1)
                n = r // 4 * P
                pe.matmul(psXC[base % 2][:, 0:n], center[:, :], xTs[:, base % 2, 0:n], start=True, stop=True)\
                  .then_inc(s["xc_ready"], 1)

            def products(c, base):
                _, p, r = CH[base]
                pe.wait_ge(s["rs_done"], c + 1)
                if base >= 2:
                    pe.wait_ge(s["std_done"], c - 1)
                    pe.wait_ge(s["y_used"], c - 1)
                for g in range(r // 4):
                    m = pe.matmul(psV[base % 2][0:p, 4 * g:4 * g + 4], sqT[:, base % 2, g * P:g * P + p], ones_g[:, :],
                                  start=True, stop=True)
                m.then_inc(s["v_ready"], 1)
                for g in range(r // 4):
                    m = pe.matmul(psY[base % 2][0:p, g * P:(g + 1) * P], rT[:, base % 2, g * P:g * P + p], wself[:, :],
                                  start=True, stop=True)
                m.then_inc(s["y_ready"], 1)

            def node_step(c, base):
                if base < NCH:
                    transposes(c, base)
                if 1 <= base <= NCH:
                    centre(c - 1, base - 1)
                if 2 <= base <= NCH + 1:
                    if base == 2:
                        pe.wait_ge(s["selfw_placed"], 64)
                    products(c - 2, base - 2)

            pe.wait_ge(s["pool_const"], 2)
            pe.wait_ge(s["dve_const"], 2)
            for k in range(DBODY):
                node_step(k, k)
            with pe.Fori(1, DLOOP) as i:
                loaded["i"] = i
                for k in range(DBODY):
                    node_step(i * DBODY + k, k + DBODY)
            for c in range(FULL, NCH + 2):
                node_step(c, c)

            def er_turn(u, k, slot, loads):
                if slot < 2:
                    pe.wait_ge(er_loaded[slot], 16 * loads)
                else:
                    pe.wait_ge(s["erlast_loaded"], 32)
                if k > 0:
                    pe.wait_ge(s["erT_copied"], u)
                pe.transpose(psER, er[slot][:, :], ident[:, :]).then_inc(s["erT_ready"], 1)

            def layer1(u, k, pairs=4):
                pe.wait_ge(s["erT_copied"], u + 1)
                if k > 0:
                    pe.wait_ge(s["x2_done"], u)
                for j in range(pairs):
                    m = pe.matmul(psMLP[:, j * P:(j + 1) * P], w1big[:, j, :], erT[:, :], start=True, stop=True)
                m.then_inc(s["l1_ready"], 1)

            def layer2(u, k, pairs=4):
                pe.wait_ge(s["x1_done"], u + 1)
                pe.matmul(psMLP[:, 0:pairs * P], w2blk[:, :], x1[:, 0:pairs * P], start=True, stop=True)\
                  .then_inc(s["l2_ready"], 1)

            def layer3(q, k, u):
                pe.wait_ge(s["x2_done"], u + 1)
                if k >= 2:
                    pe.wait_ge(s["prod_done"], q - 1)
                for h in range(2):
                    j = 2 * (k % 2) + h
                    o = psTP[k % 2][:, h * 2 * NTP:(h + 1) * 2 * NTP]
                    pe.matmul(o, x2[:, k // 2 % 2, j * P:(j + 1) * P], w3blk[:, :], start=True, stop=False)
                    m = pe.matmul(o, ones3[:, :], b3rows[:, :], start=False, stop=True)
                m.then_inc(s["tp_ready"], 1)

            def dst_rows(q, k):
                pe.wait_ge(s["dcol_done"], q + 1)
                if k >= 1:
                    pe.wait_ge(s["eq_done"], q)
                for b in range(BT):
                    m = pe.transpose(psDT[:, b * P:(b + 1) * P], dcol[:, k % 2, b:b + 1].to_broadcast([P, P]), ident[:, :])
                m.then_inc(s["dT_ready"], 1)

            def sum_batch(q, k):
                pe.wait_ge(s["msg_done"], q + 1)
                pe.wait_ge(s["eq_done"], q + 1)
                if k >= 1:
                    pe.wait_ge(s["sums_done"], q)
                for a in range(BT):
                    for b in range(a + 1):
                        o = SOFF[b] + (a - b) * P
                        m = pe.matmul(psSUM[:, a * D:(a + 1) * D], eq[:, k % 2, o:o + P], msg[:, k % 2, b, :],
                                      start=(b == 0), stop=(b == a))
                m.then_inc(s["sum_ready"], 1)

            pe.wait_ge(s["o_done"], NCH)
            pe.wait_ge(s["w_loaded"], 16 * (2 + 8 + UT))
            pe.wait_ge(s["b3_placed"], 32)
            er_turn(0, 0, 0, 1)
            dst_rows(0, 0)
            layer1(0, 0)
            layer2(0, 0)

            def edge_pass(v, first, last):
                for h in range(2):
                    u, k = 2 * v + h, (h if first else h + 4)
                    pairs = 2 if last and h == 1 else 4
                    q, kq = 2 * u, 2 * k
                    layer3(q, kq, u)
                    dst_rows(q + 1, kq + 1)
                    er_turn(u + 1, k + 1, 2 if last and h == 1 else (h + 1) % 2, v + 1 + h)
                    if not (first and h == 0):
                        sum_batch(q - 1, kq - 1)
                    layer1(u + 1, k + 1, pairs)
                    layer3(q + 1, kq + 1, u)
                    dst_rows(q + 2, kq + 2)
                    sum_batch(q, kq)
                    layer2(u + 1, k + 1, pairs)

            edge_pass(0, True, False)
            with pe.Fori(1, NU // 2 - 1) as v:
                edge_pass(v, False, False)
            edge_pass(NU // 2 - 1, False, True)
            layer3(NQ - 1, NQ - 1, NU)
            sum_batch(NQ - 2, NQ - 2)
            sum_batch(NQ - 1, NQ - 1)

        @block.vector
        def _(dve):
            for t in (er[0], er[1], er[2], w2blk, w3blk, wself, wself32):
                dve.memset(t[:, :], 0.0)
            dve.memset(w1big[:, :, :], 0.0)
            dve.memset(sh_all[:, T * 4:T * 4 + 4], 0.0)
            dve.memset(spare0[:, :], 0.0)
            dve.memset(b3rows[:, :], 0.0).then_inc(s["zeroed"], 1)
            dve.memset(epscol[:, :], EPS).then_inc(s["dve_const"], 1)
            dve.memset(ones_g[:, :], 0.0)
            dve.memset(center[:, :], 0.0)
            dve.memset(ones3[:, :], 0.0).then_inc(s["dve_zero"], 1)
            dve.wait_ge(s["dve_zero"], 1)
            dve.memset(ones3[0:3, :], 1.0)
            for g in range(4):
                dve.memset(ones_g[g * D:(g + 1) * D, g:g + 1], 1.0 / D)
                m = dve.memset(center[g * D:(g + 1) * D, g * D:(g + 1) * D], -1.0 / D)
            m.then_inc(s["dve_zero"], 1)
            dve.wait_ge(s["dve_zero"], 2)
            dve.wait_ge(s["pool_const"], 2)
            dve.tensor_tensor(center[:, :], center[:, :], ident[:, :], ALU.add).then_inc(s["dve_const"], 1)
            dve.wait_ge(s["selfw_loaded"], 64)
            dve.tensor_scalar(wself32[:, :], wself32[:, :], SELF, None, ALU.mult).then_inc(s["selfw_scaled"], 1)
            dve.wait_ge(s["w_loaded"], 16 * (2 + 8 + UT))
            for w in (w3blk, b3f):
                v = w[:, :].rearrange("p (h n) -> p h n", h=2)
                dve.tensor_scalar(v[:, :, 0:MUL * MUL], v[:, :, 0:MUL * MUL], SCALE, None, ALU.mult)
                dve.tensor_scalar(v[:, :, 2 * MUL * MUL:NTP], v[:, :, 2 * MUL * MUL:NTP], SCALE, None, ALU.mult)
                m = dve.tensor_scalar(v[:, :, MUL * MUL:2 * MUL * MUL], v[:, :, MUL * MUL:2 * MUL * MUL],
                                      SCALE * INV_SQRT3, None, ALU.mult)
                m.then_inc(s["b3_scaled"], 1)
            dve.wait_ge(s["b3_scaled"], 2)
            dve.tensor_copy(b3rows[0:1, :], b3f[:, :]).then_inc(s["b3_scaled"], 1)
            dve.wait_ge(s["b3_scaled"], 3)
            dve.tensor_tensor(b3f[:, :], b3f[:, :], b3rows[0:1, :], ALU.subtract).then_inc(s["b3_scaled"], 1)
            dve.wait_ge(s["b3_scaled"], 4)
            dve.tensor_copy(b3mid[:, :], b3f[:, :]).then_inc(s["b3_scaled"], 1)
            dve.wait_ge(s["b3_scaled"], 5)
            dve.tensor_tensor(b3r[:, :], b3f[:, :], b3mid[:, :], ALU.subtract).then_inc(s["b3_scaled"], 1)
            dve.wait_ge(s["b3_scaled"], 6)
            dve.tensor_copy(b3lo[:, :], b3r[:, :]).then_inc(s["b3_split"], 1)

            def node_out(c, base):
                _, p, r = CH[base]
                dve.wait_ge(s["std_done"], c + 1)
                dve.reciprocal(nrstd[0:p, base % 2, 0:r], nstd[0:p, base % 2, 0:r]).then_inc(s["rstd_done"], 1)
                dve.wait_ge(s["y_ready"], c + 1)
                dve.wait_ge(s["rstd_done"], c + 1)
                if base >= XS:
                    dve.wait_ge(stored[base % XS], store_count(c, base))
                o = oc[0:p, base % XS, 0:r * D].rearrange("p (r d) -> p r d", d=D)
                dve.tensor_tensor(o, psY[base % 2][0:p, 0:r * D].rearrange("p (r d) -> p r d", d=D),
                                  nrstd[0:p, base % 2, 0:r].rearrange("p (r a) -> p r a", a=1).to_broadcast([p, r, D]),
                                  ALU.mult).then_inc(s["y_used"], 1)
                dve.wait_ge(s["y_used"], c + 1)
                dve.tensor_tensor(oc[0:p, base % XS, 0:r * D], oc[0:p, base % XS, 0:r * D], xin[0:p, base % XS, 0:r * D],
                                  ALU.add).then_inc(s["o_done"], 1)

            loop = {}

            def store_count(c, base):
                if isinstance(c, int):
                    return 16 * (c // XS)
                return loop["i"] * (16 * DBODY // XS) + 16 * ((base - DBODY) // XS)

            def feat_centre(n, slot, cnt_, w=UT):
                dve.wait_ge(gathered[slot], cnt_)
                g = xg[slot][:, 0:w * D].rearrange("p (t d) -> p t d", d=D)
                dve.tensor_reduce(gsum[:, 0:w], g, X, ALU.add).then_inc(s["gsum_done"], 1)
                dve.wait_ge(s["gsum_done"], n + 1)
                dve.scalar_tensor_tensor(out=gc[:, 0:w * D].rearrange("p (t d) -> p t d", d=D),
                                         in0=gsum[:, 0:w].rearrange("p (t a) -> p t a", a=1).to_broadcast([P, w, D]),
                                         scalar=-1.0 / D, in1=g, op0=ALU.mult, op1=ALU.add).then_inc(s["gc_done"], 1)

            def feat_var(n, w=UT):
                dve.wait_ge(s["gsq_done"], n + 1)
                dve.tensor_reduce(gvar[:, 0:w], gsq[:, 0:w * D].rearrange("p (t d) -> p t d", d=D), X, ALU.add)\
                   .then_inc(s["gvar_done"], 1)

            def feat_scale(n, w=UT):
                dve.wait_ge(s["gstd_done"], n + 1)
                dve.reciprocal(grstd[:, 0:w], gstd[:, 0:w]).then_inc(s["grstd_done"], 1)
                dve.wait_ge(s["grstd_done"], n + 1)
                dve.scalar_tensor_tensor(out=h_all[:, ds(n * (UT * D), w * D)].rearrange("p (t d) -> p t d", d=D),
                                         in0=gc[:, 0:w * D].rearrange("p (t d) -> p t d", d=D), scalar=0.0,
                                         in1=grstd[:, 0:w].rearrange("p (t a) -> p t a", a=1).to_broadcast([P, w, D]),
                                         op0=ALU.max, op1=ALU.mult).then_inc(s["h_done"], 1)

            def node_step(c, base, i, feats=True):
                if 2 <= base <= NCH + 1:
                    node_out(c - 2, base - 2)
                if feats:
                    n, slot = 2 * i + base % 8 // 4, base % 8 // 4
                    if base % 4 == 0:
                        feat_centre(n, slot, (i + 1) * (16 * UT))
                    if base % 4 == 2:
                        feat_var(n)
                    if base % 4 == 3:
                        feat_scale(n)

            for k in range(DBODY):
                node_step(k, k, 0)
            dve.wait_ge(s["pool_const"], 5)
            dve.tensor_copy(trash[:, :], trash_i[:, :])
            dve.wait_ge(s["dst_loaded"], 32)
            dve.tensor_copy(dst_f[:, :], dst_i[:, :]).then_inc(s["dst_cast"], 1)
            with dve.Fori(1, DLOOP) as i:
                loop["i"] = i
                for k in range(DBODY):
                    node_step(i * DBODY + k, k + DBODY, i)
            for c in range(FULL, NCH + 2):
                node_step(c, c, 0, False)

            def dst_cols(q, k):
                if k >= 2:
                    dve.wait_ge(s["dT_ready"], q - 1)
                dve.tensor_copy(dcol[:, k % 2, :], dst_f[:, ds(q * BT, BT)]).then_inc(s["dcol_done"], 1)

            def coefs(u, k, w=UT):
                t0 = u * UT
                hs = h_all[:, ds(t0 * D, w * D)].rearrange("p (t d) -> p t d", d=D)[:, :, 0:MUL]
                hv = h_all[:, ds(t0 * D, w * D)].rearrange("p (t d) -> p t d", d=D)[:, :, MUL:D]
                sh = sh_all[:, ds(t0 * 4, w * 4)].rearrange("p (t k) -> p t k", k=4)
                c = coef[:, k % 2, 0:w, :]
                dp = dotp[:, 0:w * 24].rearrange("p (t u i) -> p t u i", u=MUL, i=3)
                dve.tensor_tensor(dp, hv.rearrange("p t (u i) -> p t u i", i=3),
                                  sh[:, :, 1:4].rearrange("p t (a i) -> p t a i", a=1).to_broadcast([P, w, MUL, 3]),
                                  ALU.mult)
                m = dve.tensor_tensor(c[:, :, 0:MUL], hs, sh[:, :, 0:1].to_broadcast([P, w, MUL]), ALU.mult)
                m.then_inc(s["dot_done"], 1)
                dve.tensor_tensor(c[:, :, 3 * MUL:6 * MUL].rearrange("p t (i u) -> p t i u", i=3),
                                  hv.rearrange("p t (u i) -> p t i u", i=3),
                                  sh[:, :, 0:1].rearrange("p t (a i) -> p t a i", a=1).to_broadcast([P, w, 3, MUL]),
                                  ALU.mult)
                dve.tensor_copy(c[:, :, 2 * MUL:3 * MUL], hs)
                dve.wait_ge(s["dot_done"], u + 1)
                dve.tensor_reduce(c[:, :, MUL:2 * MUL], dp, X, ALU.add).then_inc(s["coef_done"], 1)

            def compare(q, k):
                dve.wait_ge(s["dT_ready"], q + 1)
                if k >= 2:
                    dve.wait_ge(s["sum_ready"], q - 1)
                for b in range(BT):
                    w = (BT - b) * P
                    m = dve.scalar_tensor_tensor(out=eq[:, k % 2, SOFF[b]:SOFF[b + 1]], in0=psDT[:, b * P:BT * P],
                                                 scalar=dcol[:, k % 2, b:b + 1], in1=later[:, 0:w],
                                                 op0=ALU.is_equal, op1=ALU.mult, accum_out=cnt[:, b:b + 1])
                m.then_inc(s["eq_done"], 1)

            def indices(q, k):
                dve.tensor_tensor(dmt[:, :], dcol[:, k % 2, :], trash[:, :], ALU.subtract).then_inc(s["dmt_done"], 1)
                dve.wait_ge(s["eq_done"], q + 1)
                dve.tensor_scalar(win[:, :], cnt[:, :], 1.5, None, ALU.is_lt).then_inc(s["win_done"], 1)
                dve.wait_ge(s["win_done"], q + 1)
                dve.tensor_tensor(idx_f[:, :], win[:, :], dmt[:, :], ALU.mult).then_inc(s["idxf_done"], 1)
                dve.wait_ge(s["idxf_done"], q + 1)
                if k >= NS:
                    dve.wait_ge(s["scattered"], (q - NS + 1) * 16 * BT)
                dve.tensor_tensor(idx_i[:, k % NS, :], idx_f[:, :], trash[:, :], ALU.add).then_inc(s["idx_done"], 1)

            def messages(q, k, u):
                r = k % 2
                w = psTP[k % 2].rearrange("p (t n) -> p t n", n=NTP)
                c = coef[:, k // 2 % 2, r * BT:(r + 1) * BT, :]
                dve.wait_ge(s["tp_ready"], q + 1)
                dve.wait_ge(s["coef_done"], u + 1)
                dve.tensor_tensor(prod[:, :, 0:192].rearrange("p t (g w) -> p t g w", w=MUL),
                                  w[:, :, 0:192].rearrange("p t (g w) -> p t g w", w=MUL),
                                  c[:, :, 0:24].rearrange("p t (g a) -> p t g a", a=1).to_broadcast([P, BT, 24, MUL]), ALU.mult)
                for i in range(3):
                    m = dve.tensor_tensor(prod[:, :, 192 + 64 * i:256 + 64 * i].rearrange("p t (g w) -> p t g w", w=MUL),
                                          w[:, :, 192:256].rearrange("p t (g w) -> p t g w", w=MUL),
                                          c[:, :, 24 + 8 * i:32 + 8 * i].rearrange("p t (g a) -> p t g a", a=1)
                                          .to_broadcast([P, BT, MUL, MUL]), ALU.mult)
                m.then_inc(s["prod_done"], 1)
                dve.wait_ge(s["prod_done"], q + 1)
                dve.tensor_reduce(red[:, :, :, :].rearrange("p t g w -> p (t g) w"),
                                  prod[:, :, :].rearrange("p t (g u w) -> p (t g) w u", u=MUL, w=MUL), X, ALU.add)\
                   .then_inc(s["red_done"], 1)
                dve.wait_ge(s["red_done"], q + 1)
                if k >= 2:
                    dve.wait_ge(s["sum_ready"], q - 1)
                sh1 = sh_all[:, ds(q * (BT * 4), BT * 4)].rearrange("p (t k) -> p t k", k=4)[:, :, 1:4]
                dve.tensor_tensor(outer[:, :, :].rearrange("p t (w i) -> p t w i", i=3),
                                  red[:, :, 2, :].rearrange("p t (w a) -> p t w a", a=1).to_broadcast([P, BT, MUL, 3]),
                                  sh1.rearrange("p t (a i) -> p t a i", a=1).to_broadcast([P, BT, MUL, 3]), ALU.mult)\
                   .then_inc(s["outer_done"], 1)
                dve.tensor_tensor(msg[:, k % 2, :, 0:MUL], red[:, :, 0, :], red[:, :, 1, :], ALU.add)
                dve.wait_ge(s["outer_done"], q + 1)
                dve.tensor_tensor(msg[:, k % 2, :, MUL:D].rearrange("p t (w i) -> p t w i", i=3),
                                  outer[:, :, :].rearrange("p t (w i) -> p t w i", i=3),
                                  red[:, :, 3:6, :].rearrange("p t i w -> p t w i"), ALU.add).then_inc(s["msg_done"], 1)

            dve.wait_ge(s["dst_cast"], 1)
            dve.wait_ge(s["sh_loaded"], 32)
            dve.wait_ge(s["pool_const"], 5)
            dst_cols(0, 0)
            dst_cols(1, 1)

            def edge_pass(v, first, last):
                n = EARLY + v
                feat_centre(n, 2, (v + 1) * (16 * UT))
                for h in range(2):
                    u, ku = 2 * v + h, (h if first else h + 4)
                    dve.wait_ge(s["h_done"], n + h)
                    coefs(u, ku)
                    for r in range(2):
                        q, k = 2 * u + r, 2 * ku + r
                        dve.wait_ge(s["dcol_done"], q + 1)
                        compare(q, k)
                        indices(q, k)
                        if h == 0 and r == 0:
                            feat_var(n)
                        if h == 0 and r == 1:
                            feat_scale(n)
                        if not (last and h == 1 and r == 1):
                            dst_cols(q + 2, k + 2)
                        messages(q, k, u)

            edge_pass(0, True, False)
            with dve.Fori(1, NU // 2 - 1) as v:
                edge_pass(v, False, False)
            edge_pass(NU // 2 - 1, False, True)
            feat_centre(NU, 2, (NU // 2) * 16 * UT + 16 * BT, BT)
            q = NQ - 1
            dve.wait_ge(s["dcol_done"], q + 1)
            compare(q, q)
            indices(q, q)
            feat_var(NU, BT)
            feat_scale(NU, BT)
            dve.wait_ge(s["h_done"], NU + 1)
            coefs(NU, NU, BT)
            messages(q, q, NU)


_INS = ["x", "src", "dst", "edge_attr_4", "edge_attr_8", "L0_gnn_W1", "L0_gnn_b1", "L0_gnn_W2", "L0_gnn_b2",
        "L0_gnn_W3", "L0_gnn_b3", "L0_gnn_Ws", "L0_gnn_Wv"]


def kernel(**inputs):
    import numpy as _np
    import concourse.bacc as _bacc
    from concourse import mybir as _mybir
    from concourse.bass_utils import run_bass_kernel_spmd as _run

    nc = _bacc.Bacc("TRN2", target_bir_lowering=False, num_devices=1)
    arrays, args = {}, []
    for name in _INS:
        a = _np.ascontiguousarray(inputs[name])
        arrays[f"in_{name}_dram"] = a
        args.append(nc.dram_tensor(f"in_{name}_dram", a.shape, _mybir.dt.from_np(a.dtype), kind="ExternalInput").ap())
    n, d = inputs["x"].shape
    spare = 4 * 128
    args.append(nc.dram_tensor("out_dram", (n + spare, d), _mybir.dt.float32, kind="ExternalOutput").ap())
    gnn_layer(nc, *args)
    r = _run(nc, [arrays], core_ids=[0])
    return r.results[0]["out_dram"][:n]
```

```python
import numpy as np
import concourse.bass as bass
from concourse import mybir
from contextlib import ExitStack


def gnn_layer(nc, x, src, dst, edge_sh, edge_radial, W1, b1, W2, b2, W3, b3, Ws, Wv, out):
    f32, bf16, i32 = mybir.dt.float32, mybir.dt.bfloat16, mybir.dt.int32
    ALU = mybir.AluOpType
    ACT = mybir.ActivationFunctionType
    X = mybir.AxisListType.X
    ds = bass.ds

    P = 128
    N, D = x.shape
    E = src.shape[0]
    MUL = Ws.shape[0]
    NB, HR = W1.shape
    NTP = W3.shape[1]
    EPS = 1e-5
    SCALE = float(1.0 / np.sqrt(2.0 * MUL) / np.sqrt(16.0))
    INV_SQRT3 = float(1.0 / np.sqrt(3.0))
    SELF = float(1.0 / np.sqrt(MUL))

    R = 16
    FULL = N // (P * R)
    CH = [(c * P * R, P, R) for c in range(FULL)]
    rest = N - FULL * P * R
    R2 = rest // P // 4 * 4
    CH.append((FULL * P * R, P, R2))
    P3 = (rest - R2 * P) // 4
    CH.append((FULL * P * R + R2 * P, P3, 4))
    NCH = len(CH)
    XS = 8
    DBODY = 8
    DLOOP = FULL // DBODY

    T = E // P
    TAIL = E - T * P
    UT, BT = 8, 4
    NU = T // UT
    NQ = 2 * NU + 1
    assert T + 1 == NU * UT + BT and TAIL > 0
    EARLY = NU // 2
    assert EARLY * 4 == FULL
    DR = D + 1
    SOFF = [0, 512, 896, 1152, 1280]
    FILL = [[], [0, 1, 2], [3, 4, 5], [6, 7]]
    NS = 4

    x_v = x
    er_main = edge_radial[0:T * P, :].rearrange("(p t) k -> p (t k)", p=P)
    sh_main = edge_sh[0:T * P, :].rearrange("(p t) k -> p (t k)", p=P)
    dst_main = dst[0:T * P].rearrange("(p t) -> p t", p=P)
    src_main = src[0:T * P].rearrange("(p t) -> p t", p=P)

    ctx = ExitStack()
    with ctx:
        def sb(name, shape, dt=f32):
            return ctx.enter_context(nc.sbuf_tensor(name, shape, dt))

        def sem(name):
            return ctx.enter_context(nc.semaphore(name))

        ident = sb("ident", [P, P])
        center = sb("center", [P, P])
        ones_g = sb("ones_g", [P, 4])
        wself = sb("wself", [P, P])
        wself32 = sb("wself32", [D, D])
        w1big = sb("w1big", [P, 4, P])
        w2blk = sb("w2blk", [P, P])
        w3blk = sb("w3blk", [P, 2 * NTP])
        b1col = sb("b1col", [P, 1])
        b2col = sb("b2col", [P, 1])
        epscol = sb("epscol", [P, 1])
        b3f = sb("b3f", [1, 2 * NTP])
        b3r = sb("b3r", [1, 2 * NTP])
        b3mid = sb("b3mid", [1, 2 * NTP], bf16)
        b3lo = sb("b3lo", [1, 2 * NTP], bf16)
        b3rows = sb("b3rows", [P, 2 * NTP], bf16)
        ones3 = sb("ones3", [P, P], bf16)
        rank_w = sb("rank_w", [P, 1], i32)
        rank_max = sb("rank_max", [P, 1])
        trash_i = sb("trash_i", [P, BT], i32)
        trash = sb("trash", [P, BT])
        spare0 = sb("spare0", [P, D * 4])
        xin = sb("xin", [P, XS, R * D])
        oc = sb("oc", [P, XS, R * D])
        xTs = sb("xTs", [P, 2, R * D])
        rT = sb("rT", [P, 2, R * D])
        sqT = sb("sqT", [P, 2, R * D])
        nstd = sb("nstd", [P, 2, R])
        nrstd = sb("nrstd", [P, 2, R])
        src_slot = [sb(f"src_slot{i}", [P, UT], i32) for i in range(3)]
        xg = [sb(f"xg{i}", [P, UT * D]) for i in range(3)]
        gsum = sb("gsum", [P, UT])
        gc = sb("gc", [P, UT * D])
        gsq = sb("gsq", [P, UT * D])
        gvar = sb("gvar", [P, UT])
        gstd = sb("gstd", [P, UT])
        grstd = sb("grstd", [P, UT])
        h_all = sb("h_all", [P, (T + 1) * D])
        sh_all = sb("sh_all", [P, (T + 1) * 4])
        dst_i = sb("dst_i", [P, T + 1], i32)
        dst_f = sb("dst_f", [P, T + 1])
        er = [sb(f"er{i}", [P, P]) for i in range(3)]
        erT = sb("erT", [P, P])
        x1 = sb("x1", [P, 4 * P])
        x2 = sb("x2", [P, 2, 4 * P])
        coef = sb("coef", [P, 2, UT, 6 * MUL])
        dotp = sb("dotp", [P, UT * 3 * MUL])
        prod = sb("prod", [P, BT, 6 * 64])
        red = sb("red", [P, BT, 6, MUL])
        outer = sb("outer", [P, BT, 3 * MUL])
        msg = sb("msg", [P, 2, BT, DR])
        dcol = sb("dcol", [P, 2, BT])
        eq = sb("eq", [P, 2, SOFF[4]])
        dts = sb("dts", [P, 2, BT * P])
        lcnt = sb("lcnt", [P, 2, BT])
        lone = sb("lone", [P, 2, SOFF[4]])
        dmt_all = sb("dmt_all", [P, T + 1])
        first = sb("first", [P, BT])
        idx_f = sb("idx_f", [P, BT])
        idx_i = sb("idx_i", [P, NS, BT], i32)
        sums = sb("sums", [P, NS, BT * DR])

        ps = ctx.enter_context(nc.psum_tensor("ps", [P, 8 * 512], f32))

        def bank(b, n=1):
            return ps[:, b * 512:(b + n) * 512]

        psXT = [bank(0), bank(1)]
        psXC = [bank(2), bank(3)]
        psY = [bank(4), bank(5)]
        psV = [bank(6)[:, 0:R], bank(7)[:, 0:R]]
        psTP = [bank(0, 2), bank(2, 2)]
        psMLP = bank(4)
        psER = bank(5)[:, 0:P]
        psDT = bank(6)
        psSUM = bank(7)[:, 0:BT * DR]

        names = """zeroed w_loaded selfw_loaded selfw_scaled selfw_placed pool_const dve_const b3_split b3_placed
            spare_stored dst_pad dst_loaded dst_cast sh_loaded
            xT_ready xT_copied xc_ready rs_done v_ready y_ready std_done rstd_done y_used o_done
            gsum_done gc_done gsq_done gvar_done gstd_done grstd_done h_done
            erT_ready erT_copied l1_ready x1_done l2_ready x2_done
            dot_done coef_done tp_ready prod_done red_done outer_done msg_done
            dcol_done dT_ready dT_copied eq_done lcnt_done first_done idxf_done idx_done
            sum_ready sums_done scattered erlast_loaded dve_zero b3_scaled""".split()
        s = {n: sem(n) for n in names}
        x_loaded = [sem(f"x_loaded{i}") for i in range(XS)]
        stored = [sem(f"stored{i}") for i in range(XS)]
        src_loaded = [sem(f"src_loaded{i}") for i in range(3)]
        gathered = [sem(f"gathered{i}") for i in range(3)]
        er_loaded = [sem(f"er_loaded{i}") for i in range(2)]

        def rows(ap, c, base):
            _, p, r = CH[min(base, NCH - 1)]
            r0 = c * (P * R) if base < FULL else CH[base][0]
            return ap[ds(r0, p * r), :].rearrange("(p r) d -> p (r d)", p=p), p, r * D

        block = ctx.enter_context(nc.Block())

        @block.sync
        def _(sp):
            def load_src(u, slot):
                sp.dma_start(src_slot[slot][:, :], src_main[:, ds(u * UT, UT)]).then_inc(src_loaded[slot], 16)

            def load_er(u, slot):
                sp.dma_start(er[slot][:, 0:UT * NB], er_main[:, ds(u * UT * NB, UT * NB)])\
                  .then_inc(er_loaded[slot], 16)

            def load_x(c, base):
                if base >= XS:
                    sp.wait_ge(s["o_done"], c - XS + 1)
                v, p, n = rows(x_v, c, base)
                sp.dma_start(xin[0:p, base % XS, 0:n], v).then_inc(x_loaded[base % XS], 16)

            def store(c, base):
                sp.wait_ge(s["o_done"], c + 1)
                v, p, n = rows(out, c, base)
                sp.dma_start(v, oc[0:p, base % XS, 0:n]).then_inc(stored[base % XS], 16)

            load_src(0, 0)
            load_src(1, 1)
            for c in range(4):
                load_x(c, c)
            load_src(EARLY + 1, 2)
            sp.dma_start(dst_i[:, 0:T], dst_main).then_inc(s["dst_loaded"], 16)
            sp.dma_start(sh_all[:, 0:T * 4], sh_main).then_inc(s["sh_loaded"], 16)
            for c in range(4, XS):
                load_x(c, c)
            sp.wait_ge(s["zeroed"], 1)
            load_er(0, 0)
            load_er(1, 1)
            lt = T - NU * UT
            sp.dma_start(er[2][:, 0:lt * NB], er_main[:, NU * UT * NB:T * NB]).then_inc(s["erlast_loaded"], 16)
            sp.dma_start(er[2][0:TAIL, lt * NB:(lt + 1) * NB], edge_radial[T * P:E, :]).then_inc(s["erlast_loaded"], 16)
            sp.dma_start(sh_all[0:TAIL, T * 4:T * 4 + 4], edge_sh[T * P:E, :]).then_inc(s["sh_loaded"], 16)
            sp.wait_ge(s["dst_pad"], 1)
            sp.dma_start(dst_i[0:TAIL, T:T + 1], dst[T * P:E].rearrange("(n a) -> n a", a=1)).then_inc(s["dst_loaded"], 16)
            sp.dma_start(out[N:N + BT * P, :].rearrange("(p r) d -> p (r d)", p=P), spare0[:, :]).then_inc(s["spare_stored"], 16)

            def node_pass(i, first):
                for k in range(DBODY):
                    c = i * DBODY + k
                    base = k if first else k + DBODY
                    if base >= XS:
                        store(c - XS, base - XS)
                        load_x(c, base)
                    if k in (3, 7):
                        slot = k // 4
                        sp.wait_ge(gathered[slot], (i + 1) * 16 * UT)
                        load_src(2 * i + 2 + slot, slot)

            node_pass(0, True)
            with sp.Fori(1, DLOOP - 1) as i:
                node_pass(i, False)
            for k in range(DBODY):
                c = (DLOOP - 1) * DBODY + k
                store(c - XS, c - XS)
                load_x(c, c)
                if k == 3:
                    sp.wait_ge(gathered[0], (EARLY // 2) * 16 * UT)
                    load_src(EARLY, 0)
            for c in range(FULL, NCH):
                store(c - XS, c - XS)
                load_x(c, c)
            for c in range(NCH - XS, NCH):
                store(c, c)

            def edge_pass(v, src_too=True):
                if src_too:
                    sp.wait_ge(gathered[2], (v + 1) * 16 * UT)
                    load_src(EARLY + 2 + v, 2)
                for h in range(2):
                    sp.wait_ge(s["erT_ready"], 2 * v + h + 1)
                    load_er(2 * v + 2 + h, h)

            with sp.Fori(0, NU // 2 - 2) as v:
                edge_pass(v)
            v = NU // 2 - 2
            sp.wait_ge(gathered[2], (v + 1) * 16 * UT)
            sp.dma_start(src_slot[2][:, 0:lt], src_main[:, NU * UT:T]).then_inc(src_loaded[2], 16)
            sp.dma_start(src_slot[2][0:TAIL, lt:lt + 1], src[T * P:E].rearrange("(n a) -> n a", a=1)).then_inc(src_loaded[2], 16)
            edge_pass(v, False)

        @block.gpsimd
        def _(pool):
            pool.memset(ident[:, :], 0.0).then_inc(s["pool_const"], 1)
            pool.wait_ge(s["pool_const"], 1)
            pool.affine_select(out=ident[:, :], in_=ident[:, :], compare_op=ALU.not_equal, fill=1.0, base=0,
                               pattern=[[-1, P]], channel_multiplier=1).then_inc(s["pool_const"], 1)

            def gather(t, slot):
                pool.indirect_dma_start(xg[slot][:, t * D:(t + 1) * D], None, x,
                                        bass.IndirectOffsetOnAxis(ap=src_slot[slot][:, t:t + 1], axis=0))\
                    .then_inc(gathered[slot], 16)

            def gather_early(i, first):
                for slot in range(2):
                    pool.wait_ge(src_loaded[slot], 16 * (i + 1))
                    if not first:
                        pool.wait_ge(s["gc_done"], 2 * i + slot - 1)
                        pool.nop(nofuse=True)
                    for t in range(UT):
                        gather(t, slot)

            gather_early(0, True)
            pool.iota(rank_w[:, :], pattern=[[1, 1]], base=(127 + 63) << 23, channel_multiplier=-(1 << 23))\
                .then_inc(s["pool_const"], 1)
            pool.iota(trash_i[:, :], pattern=[[P, BT]], base=N, channel_multiplier=1).then_inc(s["pool_const"], 1)
            pool.iota(dst_i[:, T:T + 1], pattern=[[1, 1]], base=N + (BT - 1) * P, channel_multiplier=1)\
                .then_inc(s["dst_pad"], 1)
            with pool.Fori(1, EARLY // 2) as i:
                gather_early(i, False)
            pool.wait_ge(src_loaded[0], 16 * (EARLY // 2 + 1))
            pool.wait_ge(s["gc_done"], EARLY - 1)
            for t in range(UT):
                gather(t, 0)
            pool.wait_ge(src_loaded[2], 16)
            for t in range(UT):
                gather(t, 2)

            def scatter(q, k):
                pool.wait_ge(s["idx_done"], q + 1)
                if k != 0:
                    pool.wait_ge(s["scattered"], q * 16 * BT)
                pool.nop(nofuse=True)
                for a in range(BT):
                    pool.indirect_dma_start(out, bass.IndirectOffsetOnAxis(ap=idx_i[:, k % NS, a:a + 1], axis=0),
                                            sums[:, k % NS, a * DR:a * DR + D], None, compute_op=ALU.add)\
                        .then_inc(s["scattered"], 16)

            def edge_pass(v, first, tiles):
                for k in range(4):
                    if k == 1 and tiles:
                        pool.wait_ge(src_loaded[2], 16 * (v + 2) + (16 if tiles < UT else 0))
                        pool.wait_ge(s["gc_done"], EARLY + v + 2)
                        pool.nop(nofuse=True)
                    for t in FILL[k]:
                        if t < tiles:
                            gather(t, 2)
                    scatter(4 * v + k, k if first else k + 4)

            for k in range(XS):
                pool.wait_ge(stored[k], 16 * len(range(k, NCH, XS)))
            pool.wait_ge(s["spare_stored"], 16)
            edge_pass(0, True, UT)
            with pool.Fori(1, NU // 2 - 2) as v:
                edge_pass(v, False, UT)
            edge_pass(NU // 2 - 2, False, BT)
            edge_pass(NU // 2 - 1, False, 0)
            scatter(NQ - 1, NQ - 1)
            pool.wait_ge(s["scattered"], NQ * 16 * BT)

        @block.scalar
        def _(act):
            def copy_xT(c, base):
                _, p, r = CH[base]
                n = r // 4 * P if base >= FULL else R * D
                act.wait_ge(s["xT_ready"], c + 1)
                if base >= 2:
                    act.wait_ge(s["xc_ready"], c - 1)
                act.activation(xTs[:, base % 2, 0:n], psXT[base % 2][:, 0:n], ACT.Copy).then_inc(s["xT_copied"], 1)

            def relu_square(c, base):
                _, p, r = CH[base]
                n = r // 4 * P if base >= FULL else R * D
                act.wait_ge(s["xc_ready"], c + 1)
                if base >= 2:
                    act.wait_ge(s["y_ready"], c - 1)
                act.activation(sqT[:, base % 2, 0:n], psXC[base % 2][:, 0:n], ACT.Square)
                act.activation(rT[:, base % 2, 0:n], psXC[base % 2][:, 0:n], ACT.Relu).then_inc(s["rs_done"], 1)

            def node_std(c, base):
                _, p, r = CH[base]
                act.wait_ge(s["v_ready"], c + 1)
                if base >= 2:
                    act.wait_ge(s["rstd_done"], c - 1)
                act.activation(nstd[0:p, base % 2, 0:r], psV[base % 2][0:p, 0:r], ACT.Sqrt,
                               bias=epscol[0:p, :]).then_inc(s["std_done"], 1)

            def feat_square(n, w=UT * D):
                act.wait_ge(s["gc_done"], n + 1)
                act.activation(gsq[:, 0:w], gc[:, 0:w], ACT.Square).then_inc(s["gsq_done"], 1)

            def feat_std(n, w=UT):
                act.wait_ge(s["gvar_done"], n + 1)
                act.activation(gstd[:, 0:w], gvar[:, 0:w], ACT.Sqrt, bias=epscol[:, :], scale=1.0 / D)\
                   .then_inc(s["gstd_done"], 1)

            act.wait_ge(s["zeroed"], 1)
            act.dma_start(wself32[0:MUL, 0:MUL], Ws).then_inc(s["selfw_loaded"], 16)
            for i in range(3):
                with nc.allow_non_contiguous_dma(reason="64 weights"):
                    act.dma_start(wself32[MUL + i:D:3, MUL + i:D:3], Wv).then_inc(s["selfw_loaded"], 16)
            act.wait_ge(s["selfw_scaled"], 1)
            for g in range(4):
                act.dma_start(wself[g * D:(g + 1) * D, g * D:(g + 1) * D], wself32[:, :]).then_inc(s["selfw_placed"], 16)
            act.wait_ge(s["dve_const"], 1)

            def node_step(c, base, i, feats=True):
                if base < NCH:
                    copy_xT(c, base)
                if 1 <= base <= NCH:
                    relu_square(c - 1, base - 1)
                if 2 <= base <= NCH + 1:
                    node_std(c - 2, base - 2)
                if feats and base % 4 == 1:
                    feat_square(2 * i + base % 8 // 4)
                if feats and base % 4 == 3:
                    feat_std(2 * i + base % 8 // 4)

            for k in range(DBODY):
                node_step(k, k, 0)
                if k == 1:
                    act.dma_start(b3f[:, 0:NTP], b3.rearrange("(a n) -> a n", a=1)).then_inc(s["w_loaded"], 16)
                    act.dma_start(b3f[:, NTP:2 * NTP], b3.rearrange("(a n) -> a n", a=1)).then_inc(s["w_loaded"], 16)
                    for h in range(2):
                        act.dma_start(w3blk[h * HR:(h + 1) * HR, h * NTP:(h + 1) * NTP], W3).then_inc(s["w_loaded"], 16)
                        act.dma_start(w2blk[h * HR:(h + 1) * HR, h * HR:(h + 1) * HR], W2).then_inc(s["w_loaded"], 16)
                        act.dma_start(b1col[h * HR:(h + 1) * HR, :], b1.rearrange("(n a) -> n a", a=1)).then_inc(s["w_loaded"], 16)
                        act.dma_start(b2col[h * HR:(h + 1) * HR, :], b2.rearrange("(n a) -> n a", a=1)).then_inc(s["w_loaded"], 16)
                    for t in range(UT):
                        act.dma_start(w1big[t * NB:(t + 1) * NB, t // 2, (t % 2) * HR:(t % 2 + 1) * HR], W1)\
                           .then_inc(s["w_loaded"], 16)
                if k == 6:
                    act.wait_ge(s["b3_split"], 1)
                    act.dma_start(b3rows[1:2, :], b3mid[:, :]).then_inc(s["b3_placed"], 16)
                    act.dma_start(b3rows[2:3, :], b3lo[:, :]).then_inc(s["b3_placed"], 16)
            with act.Fori(1, DLOOP) as i:
                for k in range(DBODY):
                    node_step(i * DBODY + k, k + DBODY, i)
            for c in range(FULL, NCH + 2):
                node_step(c, c, DLOOP)

            def mlp_in(u, k):
                act.wait_ge(s["erT_ready"], u + 1)
                if k > 0:
                    act.wait_ge(s["l1_ready"], u)
                act.activation(erT[:, :], psER, ACT.Copy).then_inc(s["erT_copied"], 1)

            def mlp_one(u, k, w=4 * P):
                act.wait_ge(s["l1_ready"], u + 1)
                if k > 0:
                    act.wait_ge(s["l2_ready"], u)
                act.activation(x1[:, 0:w], psMLP[:, 0:w], ACT.Silu, bias=b1col[:, :]).then_inc(s["x1_done"], 1)

            def mlp_two(u, k, w=4 * P):
                act.wait_ge(s["l2_ready"], u + 1)
                if k > 1:
                    act.wait_ge(s["tp_ready"], 2 * u - 2)
                act.activation(x2[:, k % 2, 0:w], psMLP[:, 0:w], ACT.Silu, bias=b2col[:, :]).then_inc(s["x2_done"], 1)

            def copy_sums(q, k):
                act.wait_ge(s["sum_ready"], q + 1)
                if k >= NS:
                    act.wait_ge(s["scattered"], (q - NS + (2 if k % NS == NS - 1 else 1)) * 16 * BT)
                act.activation(sums[:, k % NS, :], psSUM, ACT.Copy).then_inc(s["sums_done"], 1)

            def dst_col(q, k):
                if k >= 2:
                    act.wait_ge(s["dT_ready"], q - 1)
                    act.wait_ge(s["eq_done"], q - 1)
                act.activation(dcol[:, k % 2, :], dst_f[:, ds(q * BT, BT)], ACT.Copy).then_inc(s["dcol_done"], 1)

            def dst_copy(q, k):
                act.wait_ge(s["dT_ready"], q + 1)
                if k >= 2:
                    act.wait_ge(s["eq_done"], q - 1)
                act.activation(dts[:, k % 2, :], psDT, ACT.Copy).then_inc(s["dT_copied"], 1)

            def later_count(q, k):
                act.wait_ge(s["eq_done"], q + 1)
                if k >= 2:
                    act.wait_ge(s["idx_done"], q - 1)
                for b in range(BT - 1):
                    m = act.activation(lone[:, k % 2, SOFF[b] + P:SOFF[b + 1]], eq[:, k % 2, SOFF[b] + P:SOFF[b + 1]], ACT.Copy,
                                       accum_out=lcnt[:, k % 2, b:b + 1])
                m.then_inc(s["lcnt_done"], 1)

            act.wait_ge(s["dst_cast"], 1)
            dst_col(0, 0)
            dst_col(1, 1)
            act.wait_ge(s["w_loaded"], 16 * (2 + 8 + UT))
            mlp_in(0, 0)
            mlp_one(0, 0)
            mlp_two(0, 0)
            dst_copy(0, 0)

            def edge_pass(v, first, last):
                n = EARLY + 1 + v
                fw, fn = (BT * D, BT) if last else (UT * D, UT)
                for h in range(2):
                    u, k = 2 * v + h, (h if first else h + 4)
                    q, kq = 2 * u, 2 * k
                    w = 2 * P if last and h == 1 else 4 * P
                    mlp_in(u + 1, k + 1)
                    dst_copy(q + 1, kq + 1)
                    mlp_one(u + 1, k + 1, w)
                    if not (first and h == 0):
                        copy_sums(q - 1, kq - 1)
                    later_count(q, kq)
                    dst_col(q + 2, kq + 2)
                    if h == 1:
                        feat_square(n, fw)
                    dst_copy(q + 2, kq + 2)
                    mlp_two(u + 1, k + 1, w)
                    copy_sums(q, kq)
                    later_count(q + 1, kq + 1)
                    if not (last and h == 1):
                        dst_col(q + 3, kq + 3)
                feat_std(n, fn)

            edge_pass(0, True, False)
            with act.Fori(1, NU // 2 - 1) as v:
                edge_pass(v, False, False)
            edge_pass(NU // 2 - 1, False, True)
            copy_sums(NQ - 2, NQ - 2)
            later_count(NQ - 1, NQ - 1)
            copy_sums(NQ - 1, NQ - 1)

        @block.tensor
        def _(pe):
            def transposes(c, base):
                _, p, r = CH[base]
                pe.wait_ge(x_loaded[base % XS], 16 * ((c - base % XS) // XS + 1) if isinstance(c, int)
                           else loaded_count(c, base))
                if base >= 2:
                    pe.wait_ge(s["xT_copied"], c - 1)
                for g in range(r // 4):
                    m = pe.transpose(psXT[base % 2][:, g * P:g * P + p], xin[0:p, base % XS, g * P:(g + 1) * P],
                                     ident[0:p, 0:p])
                m.then_inc(s["xT_ready"], 1)

            loaded = {}

            def loaded_count(c, base):
                return loaded["i"] * (16 * DBODY // XS) + 16 * ((base - DBODY) // XS + 1)

            def centre(c, base):
                _, p, r = CH[base]
                pe.wait_ge(s["xT_copied"], c + 1)
                if base >= 2:
                    pe.wait_ge(s["rs_done"], c - 1)
                n = r // 4 * P
                pe.matmul(psXC[base % 2][:, 0:n], center[:, :], xTs[:, base % 2, 0:n], start=True, stop=True)\
                  .then_inc(s["xc_ready"], 1)

            def products(c, base):
                _, p, r = CH[base]
                pe.wait_ge(s["rs_done"], c + 1)
                if base >= 2:
                    pe.wait_ge(s["std_done"], c - 1)
                    pe.wait_ge(s["y_used"], c - 1)
                for g in range(r // 4):
                    m = pe.matmul(psV[base % 2][0:p, 4 * g:4 * g + 4], sqT[:, base % 2, g * P:g * P + p], ones_g[:, :],
                                  start=True, stop=True)
                m.then_inc(s["v_ready"], 1)
                for g in range(r // 4):
                    m = pe.matmul(psY[base % 2][0:p, g * P:(g + 1) * P], rT[:, base % 2, g * P:g * P + p], wself[:, :],
                                  start=True, stop=True)
                m.then_inc(s["y_ready"], 1)

            def node_step(c, base):
                if base < NCH:
                    transposes(c, base)
                if 1 <= base <= NCH:
                    centre(c - 1, base - 1)
                if 2 <= base <= NCH + 1:
                    if base == 2:
                        pe.wait_ge(s["selfw_placed"], 64)
                    products(c - 2, base - 2)

            pe.wait_ge(s["pool_const"], 2)
            pe.wait_ge(s["dve_const"], 2)
            for k in range(DBODY):
                node_step(k, k)
            with pe.Fori(1, DLOOP) as i:
                loaded["i"] = i
                for k in range(DBODY):
                    node_step(i * DBODY + k, k + DBODY)
            for c in range(FULL, NCH + 2):
                node_step(c, c)

            def er_turn(u, k, slot, loads):
                if slot < 2:
                    pe.wait_ge(er_loaded[slot], 16 * loads)
                else:
                    pe.wait_ge(s["erlast_loaded"], 32)
                if k > 0:
                    pe.wait_ge(s["erT_copied"], u)
                pe.transpose(psER, er[slot][:, :], ident[:, :]).then_inc(s["erT_ready"], 1)

            def layer1(u, k, pairs=4):
                pe.wait_ge(s["erT_copied"], u + 1)
                if k > 0:
                    pe.wait_ge(s["x2_done"], u)
                for j in range(pairs):
                    m = pe.matmul(psMLP[:, j * P:(j + 1) * P], w1big[:, j, :], erT[:, :], start=True, stop=True)
                m.then_inc(s["l1_ready"], 1)

            def layer2(u, k, pairs=4):
                pe.wait_ge(s["x1_done"], u + 1)
                pe.matmul(psMLP[:, 0:pairs * P], w2blk[:, :], x1[:, 0:pairs * P], start=True, stop=True)\
                  .then_inc(s["l2_ready"], 1)

            def layer3(q, k, u):
                pe.wait_ge(s["x2_done"], u + 1)
                if k >= 2:
                    pe.wait_ge(s["prod_done"], q - 1)
                for h in range(2):
                    j = 2 * (k % 2) + h
                    o = psTP[k % 2][:, h * 2 * NTP:(h + 1) * 2 * NTP]
                    pe.matmul(o, x2[:, k // 2 % 2, j * P:(j + 1) * P], w3blk[:, :], start=True, stop=False)
                    m = pe.matmul(o, ones3[:, :], b3rows[:, :], start=False, stop=True)
                m.then_inc(s["tp_ready"], 1)

            def dst_rows(q, k):
                pe.wait_ge(s["dcol_done"], q + 1)
                if k >= 1:
                    pe.wait_ge(s["dT_copied"], q)
                for b in range(BT):
                    m = pe.transpose(psDT[:, b * P:(b + 1) * P], dcol[:, k % 2, b:b + 1].to_broadcast([P, P]), ident[:, :])
                m.then_inc(s["dT_ready"], 1)

            def sum_batch(q, k):
                pe.wait_ge(s["msg_done"], q + 1)
                pe.wait_ge(s["eq_done"], q + 1)
                if k >= 1:
                    pe.wait_ge(s["sums_done"], q)
                for a in range(BT):
                    for b in [a] + list(range(a)):
                        o, n = SOFF[b] + (a - b) * P, (DR if b == a else D)
                        m = pe.matmul(psSUM[:, a * DR:a * DR + n], eq[:, k % 2, o:o + P], msg[:, k % 2, b, 0:n],
                                      start=(b == a), stop=(b == a - 1 or a == 0))
                m.then_inc(s["sum_ready"], 1)

            pe.wait_ge(s["o_done"], NCH)
            pe.wait_ge(s["w_loaded"], 16 * (2 + 8 + UT))
            pe.wait_ge(s["b3_placed"], 32)
            er_turn(0, 0, 0, 1)
            dst_rows(0, 0)
            layer1(0, 0)
            layer2(0, 0)

            def edge_pass(v, first, last):
                for h in range(2):
                    u, k = 2 * v + h, (h if first else h + 4)
                    pairs = 2 if last and h == 1 else 4
                    q, kq = 2 * u, 2 * k
                    layer3(q, kq, u)
                    dst_rows(q + 1, kq + 1)
                    er_turn(u + 1, k + 1, 2 if last and h == 1 else (h + 1) % 2, v + 1 + h)
                    if not (first and h == 0):
                        sum_batch(q - 1, kq - 1)
                    layer1(u + 1, k + 1, pairs)
                    layer3(q + 1, kq + 1, u)
                    dst_rows(q + 2, kq + 2)
                    sum_batch(q, kq)
                    layer2(u + 1, k + 1, pairs)

            edge_pass(0, True, False)
            with pe.Fori(1, NU // 2 - 1) as v:
                edge_pass(v, False, False)
            edge_pass(NU // 2 - 1, False, True)
            layer3(NQ - 1, NQ - 1, NU)
            sum_batch(NQ - 2, NQ - 2)
            sum_batch(NQ - 1, NQ - 1)

        @block.vector
        def _(dve):
            for t in (wself32, wself, er[0], er[1], er[2], w2blk, w3blk):
                dve.memset(t[:, :], 0.0)
            dve.memset(w1big[:, :, :], 0.0)
            dve.memset(lcnt[:, :, :], 0.0)
            dve.memset(sh_all[:, T * 4:T * 4 + 4], 0.0)
            dve.memset(spare0[:, :], 0.0)
            dve.memset(b3rows[:, :], 0.0).then_inc(s["zeroed"], 1)
            dve.memset(epscol[:, :], EPS).then_inc(s["dve_const"], 1)
            dve.memset(ones_g[:, :], 0.0)
            dve.memset(center[:, :], 0.0)
            dve.memset(ones3[:, :], 0.0).then_inc(s["dve_zero"], 1)
            dve.wait_ge(s["dve_zero"], 1)
            dve.memset(ones3[0:3, :], 1.0)
            for g in range(4):
                dve.memset(ones_g[g * D:(g + 1) * D, g:g + 1], 1.0 / D)
                m = dve.memset(center[g * D:(g + 1) * D, g * D:(g + 1) * D], -1.0 / D)
            m.then_inc(s["dve_zero"], 1)
            dve.wait_ge(s["dve_zero"], 2)
            dve.wait_ge(s["pool_const"], 2)
            dve.tensor_tensor(center[:, :], center[:, :], ident[:, :], ALU.add).then_inc(s["dve_const"], 1)
            dve.wait_ge(s["selfw_loaded"], 64)
            dve.tensor_scalar(wself32[:, :], wself32[:, :], SELF, None, ALU.mult).then_inc(s["selfw_scaled"], 1)
            def scale_weights():
                dve.wait_ge(s["w_loaded"], 16 * (2 + 8 + UT))
                for w in (w3blk, b3f):
                    v = w[:, :].rearrange("p (h n) -> p h n", h=2)
                    dve.tensor_scalar(v[:, :, 0:MUL * MUL], v[:, :, 0:MUL * MUL], SCALE, None, ALU.mult)
                    dve.tensor_scalar(v[:, :, 2 * MUL * MUL:NTP], v[:, :, 2 * MUL * MUL:NTP], SCALE, None, ALU.mult)
                    m = dve.tensor_scalar(v[:, :, MUL * MUL:2 * MUL * MUL], v[:, :, MUL * MUL:2 * MUL * MUL],
                                          SCALE * INV_SQRT3, None, ALU.mult)
                    m.then_inc(s["b3_scaled"], 1)
                dve.wait_ge(s["b3_scaled"], 2)
                dve.tensor_copy(b3rows[0:1, :], b3f[:, :]).then_inc(s["b3_scaled"], 1)
                dve.wait_ge(s["b3_scaled"], 3)
                dve.tensor_tensor(b3f[:, :], b3f[:, :], b3rows[0:1, :], ALU.subtract).then_inc(s["b3_scaled"], 1)
                dve.wait_ge(s["b3_scaled"], 4)
                dve.tensor_copy(b3mid[:, :], b3f[:, :]).then_inc(s["b3_scaled"], 1)
                dve.wait_ge(s["b3_scaled"], 5)
                dve.tensor_tensor(b3r[:, :], b3f[:, :], b3mid[:, :], ALU.subtract).then_inc(s["b3_scaled"], 1)
                dve.wait_ge(s["b3_scaled"], 6)
                dve.tensor_copy(b3lo[:, :], b3r[:, :]).then_inc(s["b3_split"], 1)

            def node_out(c, base):
                _, p, r = CH[base]
                dve.wait_ge(s["std_done"], c + 1)
                dve.reciprocal(nrstd[0:p, base % 2, 0:r], nstd[0:p, base % 2, 0:r]).then_inc(s["rstd_done"], 1)
                dve.wait_ge(s["y_ready"], c + 1)
                dve.wait_ge(s["rstd_done"], c + 1)
                if base >= XS:
                    dve.wait_ge(stored[base % XS], store_count(c, base))
                o = oc[0:p, base % XS, 0:r * D].rearrange("p (r d) -> p r d", d=D)
                dve.tensor_tensor(o, psY[base % 2][0:p, 0:r * D].rearrange("p (r d) -> p r d", d=D),
                                  nrstd[0:p, base % 2, 0:r].rearrange("p (r a) -> p r a", a=1).to_broadcast([p, r, D]),
                                  ALU.mult).then_inc(s["y_used"], 1)
                dve.wait_ge(s["y_used"], c + 1)
                dve.tensor_tensor(oc[0:p, base % XS, 0:r * D], oc[0:p, base % XS, 0:r * D], xin[0:p, base % XS, 0:r * D],
                                  ALU.add).then_inc(s["o_done"], 1)

            loop = {}

            def store_count(c, base):
                if isinstance(c, int):
                    return 16 * (c // XS)
                return loop["i"] * (16 * DBODY // XS) + 16 * ((base - DBODY) // XS)

            def feat_centre(n, slot, cnt_, w=UT):
                dve.wait_ge(gathered[slot], cnt_)
                g = xg[slot][:, 0:w * D].rearrange("p (t d) -> p t d", d=D)
                dve.tensor_reduce(gsum[:, 0:w], g, X, ALU.add).then_inc(s["gsum_done"], 1)
                dve.wait_ge(s["gsum_done"], n + 1)
                dve.scalar_tensor_tensor(out=gc[:, 0:w * D].rearrange("p (t d) -> p t d", d=D),
                                         in0=gsum[:, 0:w].rearrange("p (t a) -> p t a", a=1).to_broadcast([P, w, D]),
                                         scalar=-1.0 / D, in1=g, op0=ALU.mult, op1=ALU.add).then_inc(s["gc_done"], 1)

            def feat_var(n, w=UT):
                dve.wait_ge(s["gsq_done"], n + 1)
                dve.tensor_reduce(gvar[:, 0:w], gsq[:, 0:w * D].rearrange("p (t d) -> p t d", d=D), X, ALU.add)\
                   .then_inc(s["gvar_done"], 1)

            def feat_scale(n, w=UT):
                dve.wait_ge(s["gstd_done"], n + 1)
                dve.reciprocal(grstd[:, 0:w], gstd[:, 0:w]).then_inc(s["grstd_done"], 1)
                dve.wait_ge(s["grstd_done"], n + 1)
                dve.scalar_tensor_tensor(out=h_all[:, ds(n * (UT * D), w * D)].rearrange("p (t d) -> p t d", d=D),
                                         in0=gc[:, 0:w * D].rearrange("p (t d) -> p t d", d=D), scalar=0.0,
                                         in1=grstd[:, 0:w].rearrange("p (t a) -> p t a", a=1).to_broadcast([P, w, D]),
                                         op0=ALU.max, op1=ALU.mult).then_inc(s["h_done"], 1)

            def node_step(c, base, i, feats=True):
                if 2 <= base <= NCH + 1:
                    node_out(c - 2, base - 2)
                if feats:
                    n, slot = 2 * i + base % 8 // 4, base % 8 // 4
                    if base % 4 == 0:
                        feat_centre(n, slot, (i + 1) * (16 * UT))
                    if base % 4 == 2:
                        feat_var(n)
                    if base % 4 == 3:
                        feat_scale(n)

            for k in range(DBODY):
                node_step(k, k, 0)
                if k == 4:
                    scale_weights()
            dve.wait_ge(s["pool_const"], 4)
            dve.tensor_copy(trash[:, :], trash_i[:, :])
            rw = rank_w[:, :].bitcast(f32)
            dve.tensor_scalar(rank_max[:, :], rw, 2.5, None, ALU.mult)
            for k in range(2):
                for b in range(BT):
                    dve.tensor_copy(msg[:, k, b, D:DR], rw)
            dve.wait_ge(s["dst_loaded"], 32)
            dve.tensor_copy(dst_f[:, :], dst_i[:, :]).then_inc(s["dst_cast"], 1)
            dve.wait_ge(s["dst_cast"], 1)
            dve.tensor_tensor(dmt_all[:, :].rearrange("p (q t) -> p q t", t=BT),
                              dst_f[:, :].rearrange("p (q t) -> p q t", t=BT),
                              trash[:, :].rearrange("p (a t) -> p a t", a=1).to_broadcast([P, NQ, BT]), ALU.subtract)
            with dve.Fori(1, DLOOP) as i:
                loop["i"] = i
                for k in range(DBODY):
                    node_step(i * DBODY + k, k + DBODY, i)
            for c in range(FULL, NCH + 2):
                node_step(c, c, DLOOP)

            def coefs(u, k, w=UT):
                t0 = u * UT
                hs = h_all[:, ds(t0 * D, w * D)].rearrange("p (t d) -> p t d", d=D)[:, :, 0:MUL]
                hv = h_all[:, ds(t0 * D, w * D)].rearrange("p (t d) -> p t d", d=D)[:, :, MUL:D]
                sh = sh_all[:, ds(t0 * 4, w * 4)].rearrange("p (t k) -> p t k", k=4)
                c = coef[:, k % 2, 0:w, :]
                dp = dotp[:, 0:w * 24].rearrange("p (t u i) -> p t u i", u=MUL, i=3)
                dve.tensor_tensor(dp, hv.rearrange("p t (u i) -> p t u i", i=3),
                                  sh[:, :, 1:4].rearrange("p t (a i) -> p t a i", a=1).to_broadcast([P, w, MUL, 3]),
                                  ALU.mult)
                m = dve.tensor_tensor(c[:, :, 0:MUL], hs, sh[:, :, 0:1].to_broadcast([P, w, MUL]), ALU.mult)
                m.then_inc(s["dot_done"], 1)
                dve.tensor_tensor(c[:, :, 3 * MUL:6 * MUL].rearrange("p t (i u) -> p t i u", i=3),
                                  hv.rearrange("p t (u i) -> p t i u", i=3),
                                  sh[:, :, 0:1].rearrange("p t (a i) -> p t a i", a=1).to_broadcast([P, w, 3, MUL]),
                                  ALU.mult)
                dve.tensor_copy(c[:, :, 2 * MUL:3 * MUL], hs)
                dve.wait_ge(s["dot_done"], u + 1)
                dve.tensor_reduce(c[:, :, MUL:2 * MUL], dp, X, ALU.add).then_inc(s["coef_done"], 1)

            def compare(q, k):
                dve.wait_ge(s["dT_copied"], q + 1)
                if k >= 2:
                    dve.wait_ge(s["sum_ready"], q - 1)
                    dve.wait_ge(s["lcnt_done"], q - 1)
                for b in range(BT):
                    m = dve.tensor_scalar(eq[:, k % 2, SOFF[b]:SOFF[b + 1]], dts[:, k % 2, b * P:BT * P],
                                          dcol[:, k % 2, b:b + 1], None, ALU.is_equal)
                m.then_inc(s["eq_done"], 1)

            def indices(q, k):
                dve.wait_ge(s["sums_done"], q + 1)
                rank = sums[:, k % NS, :].rearrange("p (t d) -> p t d", d=DR)[:, :, D]
                dve.scalar_tensor_tensor(out=first[:, :], in0=rank, scalar=rank_max[:, :], in1=dmt_all[:, ds(q * BT, BT)],
                                         op0=ALU.is_lt, op1=ALU.mult).then_inc(s["first_done"], 1)
                dve.wait_ge(s["lcnt_done"], q + 1)
                dve.wait_ge(s["first_done"], q + 1)
                dve.scalar_tensor_tensor(out=idx_f[:, :], in0=lcnt[:, k % 2, :], scalar=0.5, in1=first[:, :],
                                         op0=ALU.is_lt, op1=ALU.mult).then_inc(s["idxf_done"], 1)
                dve.wait_ge(s["idxf_done"], q + 1)
                dve.tensor_tensor(idx_i[:, k % NS, :], idx_f[:, :], trash[:, :], ALU.add).then_inc(s["idx_done"], 1)

            def messages(q, k, u):
                r = k % 2
                w = psTP[k % 2].rearrange("p (t n) -> p t n", n=NTP)
                c = coef[:, k // 2 % 2, r * BT:(r + 1) * BT, :]
                dve.wait_ge(s["tp_ready"], q + 1)
                dve.wait_ge(s["coef_done"], u + 1)
                dve.tensor_tensor(prod[:, :, 0:192].rearrange("p t (g w) -> p t g w", w=MUL),
                                  w[:, :, 0:192].rearrange("p t (g w) -> p t g w", w=MUL),
                                  c[:, :, 0:24].rearrange("p t (g a) -> p t g a", a=1).to_broadcast([P, BT, 24, MUL]), ALU.mult)
                for i in range(3):
                    m = dve.tensor_tensor(prod[:, :, 192 + 64 * i:256 + 64 * i].rearrange("p t (g w) -> p t g w", w=MUL),
                                          w[:, :, 192:256].rearrange("p t (g w) -> p t g w", w=MUL),
                                          c[:, :, 24 + 8 * i:32 + 8 * i].rearrange("p t (g a) -> p t g a", a=1)
                                          .to_broadcast([P, BT, MUL, MUL]), ALU.mult)
                m.then_inc(s["prod_done"], 1)
                dve.wait_ge(s["prod_done"], q + 1)
                dve.tensor_reduce(red[:, :, :, :].rearrange("p t g w -> p (t g) w"),
                                  prod[:, :, :].rearrange("p t (g u w) -> p (t g) w u", u=MUL, w=MUL), X, ALU.add)\
                   .then_inc(s["red_done"], 1)
                dve.wait_ge(s["red_done"], q + 1)
                if k >= 2:
                    dve.wait_ge(s["sum_ready"], q - 1)
                sh1 = sh_all[:, ds(q * (BT * 4), BT * 4)].rearrange("p (t k) -> p t k", k=4)[:, :, 1:4]
                dve.tensor_tensor(outer[:, :, :].rearrange("p t (w i) -> p t w i", i=3),
                                  red[:, :, 2, :].rearrange("p t (w a) -> p t w a", a=1).to_broadcast([P, BT, MUL, 3]),
                                  sh1.rearrange("p t (a i) -> p t a i", a=1).to_broadcast([P, BT, MUL, 3]), ALU.mult)\
                   .then_inc(s["outer_done"], 1)
                dve.tensor_tensor(msg[:, k % 2, :, 0:MUL], red[:, :, 0, :], red[:, :, 1, :], ALU.add)
                dve.wait_ge(s["outer_done"], q + 1)
                dve.tensor_tensor(msg[:, k % 2, :, MUL:D].rearrange("p t (w i) -> p t w i", i=3),
                                  outer[:, :, :].rearrange("p t (w i) -> p t w i", i=3),
                                  red[:, :, 3:6, :].rearrange("p t i w -> p t w i"), ALU.add).then_inc(s["msg_done"], 1)

            dve.wait_ge(s["sh_loaded"], 32)

            def edge_pass(v, first, last):
                n = EARLY + 1 + v
                fw = BT if last else UT
                for h in range(2):
                    u, ku = 2 * v + h, (h if first else h + 4)
                    dve.wait_ge(s["h_done"], n)
                    coefs(u, ku)
                    for r in range(2):
                        q, k = 2 * u + r, 2 * ku + r
                        compare(q, k)
                        messages(q, k, u)
                        if not (first and h == 0 and r == 0):
                            indices(q - 1, k - 1)
                        if h == 0 and r == 1:
                            feat_centre(n, 2, (v + 1) * (16 * UT) - (16 * (UT - BT) if last else 0), fw)
                        if h == 1 and r == 0:
                            feat_var(n, fw)
                feat_scale(n, fw)

            edge_pass(0, True, False)
            with dve.Fori(1, NU // 2 - 1) as v:
                edge_pass(v, False, False)
            edge_pass(NU // 2 - 1, False, True)
            q = NQ - 1
            dve.wait_ge(s["h_done"], NU + 1)
            coefs(NU, NU, BT)
            compare(q, q)
            messages(q, q, NU)
            indices(q - 1, q - 1)
            indices(q, q)


_INS = ["x", "src", "dst", "edge_attr_4", "edge_attr_8", "L0_gnn_W1", "L0_gnn_b1", "L0_gnn_W2", "L0_gnn_b2",
        "L0_gnn_W3", "L0_gnn_b3", "L0_gnn_Ws", "L0_gnn_Wv"]


def kernel(**inputs):
    import numpy as _np
    import concourse.bacc as _bacc
    from concourse import mybir as _mybir
    from concourse.bass_utils import run_bass_kernel_spmd as _run

    nc = _bacc.Bacc("TRN2", target_bir_lowering=False, num_devices=1)
    arrays, args = {}, []
    for name in _INS:
        a = _np.ascontiguousarray(inputs[name])
        arrays[f"in_{name}_dram"] = a
        args.append(nc.dram_tensor(f"in_{name}_dram", a.shape, _mybir.dt.from_np(a.dtype), kind="ExternalInput").ap())
    n, d = inputs["x"].shape
    spare = 4 * 128
    args.append(nc.dram_tensor("out_dram", (n + spare, d), _mybir.dt.float32, kind="ExternalOutput").ap())
    gnn_layer(nc, *args)
    r = _run(nc, [arrays], core_ids=[0])
    return r.results[0]["out_dram"][:n]
```

```python
import numpy as np
import concourse.bass as bass
from concourse import mybir
from contextlib import ExitStack


def gnn_layer(nc, x, src, dst, edge_sh, edge_radial, W1, b1, W2, b2, W3, b3, Ws, Wv, out):
    f32, bf16, i32 = mybir.dt.float32, mybir.dt.bfloat16, mybir.dt.int32
    ALU = mybir.AluOpType
    ACT = mybir.ActivationFunctionType
    X = mybir.AxisListType.X
    ds = bass.ds

    P = 128
    N, D = x.shape
    E = src.shape[0]
    MUL = Ws.shape[0]
    NB, HR = W1.shape
    NTP = W3.shape[1]
    EPS = 1e-5
    SCALE = float(1.0 / np.sqrt(2.0 * MUL) / np.sqrt(16.0))
    INV_SQRT3 = float(1.0 / np.sqrt(3.0))
    SELF = float(1.0 / np.sqrt(MUL))

    R = 16
    FULL = N // (P * R)
    CH = [(c * P * R, P, R) for c in range(FULL)]
    rest = N - FULL * P * R
    R2 = rest // P // 4 * 4
    CH.append((FULL * P * R, P, R2))
    P3 = (rest - R2 * P) // 4
    CH.append((FULL * P * R + R2 * P, P3, 4))
    NCH = len(CH)
    XS = 8
    DBODY = 8
    DLOOP = FULL // DBODY

    T = E // P
    TAIL = E - T * P
    UT, BT = 8, 4
    NU = T // UT
    NQ = 2 * NU + 1
    assert T + 1 == NU * UT + BT and TAIL > 0
    EARLY = NU // 2
    assert EARLY * 4 == FULL
    DR = D + 1
    BW = BT * P
    HL = (NU // 2 - 2) // 2
    NS = 4

    er_main = edge_radial[0:T * P, :].rearrange("(p t) k -> p (t k)", p=P)
    sh_main = edge_sh[0:T * P, :].rearrange("(p t) k -> p (t k)", p=P)
    dst_main = dst[0:T * P].rearrange("(p t) -> p t", p=P)
    src_main = src[0:T * P].rearrange("(p t) -> p t", p=P)

    ctx = ExitStack()
    with ctx:
        def sb(name, shape, dt=f32):
            return ctx.enter_context(nc.sbuf_tensor(name, shape, dt))

        def sem(name):
            return ctx.enter_context(nc.semaphore(name))

        ident = sb("ident", [P, P])
        center = sb("center", [P, P])
        ones_g = sb("ones_g", [P, 4])
        wself = sb("wself", [P, P])
        wself32 = sb("wself32", [D, D])
        w1big = sb("w1big", [P, 4, P])
        w2blk = sb("w2blk", [P, P])
        w3blk = sb("w3blk", [P, 2 * NTP])
        b1col = sb("b1col", [P, 1])
        b2col = sb("b2col", [P, 1])
        epscol = sb("epscol", [P, 1])
        table_warm = sb("table_warm", [P, 1])
        onecol = sb("onecol", [P, 1])
        b3f = sb("b3f", [1, 2 * NTP])
        b3r = sb("b3r", [1, 2 * NTP])
        b3mid = sb("b3mid", [1, 2 * NTP], bf16)
        b3lo = sb("b3lo", [1, 2 * NTP], bf16)
        b3rows = sb("b3rows", [P, 2 * NTP], bf16)
        ones3 = sb("ones3", [P, P], bf16)
        rank_w = sb("rank_w", [P, 1], i32)
        rank_max = sb("rank_max", [P, 1])
        trash_i = sb("trash_i", [P, BT], i32)
        trash = sb("trash", [P, BT])
        spare0 = sb("spare0", [P, D * 4])
        xin = sb("xin", [P, XS, R * D])
        oc = sb("oc", [P, XS, R * D])
        xTs = sb("xTs", [P, 2, R * D])
        rT = sb("rT", [P, 2, R * D])
        sqT = sb("sqT", [P, 2, R * D])
        nsum = sb("nsum", [P, 2, R])
        xc = sb("xc", [P, 2, R * D])
        nstd = sb("nstd", [P, 2, R])
        nrstd = sb("nrstd", [P, 2, R])
        src_slot = [sb(f"src_slot{i}", [P, UT], i32) for i in range(3)]
        xg = [sb(f"xg{i}", [P, UT * D]) for i in range(3)]
        gsum = sb("gsum", [P, UT])
        gc = sb("gc", [P, UT * D])
        gsq = sb("gsq", [P, UT * D])
        gvar = sb("gvar", [P, UT])
        gstd = sb("gstd", [P, UT])
        grstd = sb("grstd", [P, UT])
        h_all = sb("h_all", [P, (T + 1) * D])
        sh_all = sb("sh_all", [P, (T + 1) * 4])
        dst_i = sb("dst_i", [P, T + 1], i32)
        dst_f = sb("dst_f", [P, T + 1])
        er = [sb(f"er{i}", [P, P]) for i in range(3)]
        erT = sb("erT", [P, P])
        x1 = sb("x1", [P, 4 * P])
        x2 = sb("x2", [P, 2, 4 * P])
        coef = sb("coef", [P, 2, UT, 6 * MUL])
        dotp = sb("dotp", [P, UT * 3 * MUL])
        prod = sb("prod", [P, BT, 6 * 64])
        red = sb("red", [P, BT, 4, MUL])
        outer = sb("outer", [P, BT, 3 * MUL])
        msg = sb("msg", [P, 2, BT, DR])
        dcol = sb("dcol", [P, NS, BT])
        dsq = sb("dsq", [P, BT * BW])
        eq = sb("eq", [P, 2, BT * BW])
        lcnt = sb("lcnt", [P, NS, BT])
        dmt_all = sb("dmt_all", [P, T + 1])
        first = sb("first", [P, BT])
        idx_f = sb("idx_f", [P, BT])
        idx_i = sb("idx_i", [P, NS, BT], i32)
        sums = sb("sums", [P, NS, BT * DR])

        ps = ctx.enter_context(nc.psum_tensor("ps", [P, 8 * 512], f32))

        def bank(b, n=1):
            return ps[:, b * 512:(b + n) * 512]

        psXT = [bank(0), bank(1)]
        psXC = [bank(2), bank(3)]
        psY = [bank(4), bank(5)]
        psV = [bank(6)[:, 0:R], bank(6)[:, R:2 * R]]
        psTP = [bank(0, 2), bank(2, 2)]
        psMLP = bank(7)
        psER = bank(6)[:, 0:P]
        psDT = bank(4)
        psSUM = bank(5)[:, 0:BT * DR]

        names = """selfw_zero zeroed w_loaded selfw_loaded selfw_scaled selfw_placed pool_const dve_const b3_split b3_placed
            spare_stored landed dst_pad dst_loaded dst_cast sh_loaded
            xsum_done xc_done xT_ready xT_copied xc_ready rs_done v_ready y_ready std_done rstd_done y_used o_done
            gsum_done gc_done gsq_done gvar_done gstd_done grstd_done h_done
            erT_ready erT_copied l1_ready x1_done l2_ready x2_done
            dot_done coef_done tp_ready prod_done red_done outer_done msg_done
            dcol_done dT_ready sq_done eq_done first_done idxf_done idx_done
            sum_ready sums_done scattered erlast_loaded dve_zero b3_scaled""".split()
        s = {n: sem(n) for n in names}
        x_loaded = [sem(f"x_loaded{i}") for i in range(XS)]
        stored = [sem(f"stored{i}") for i in range(XS)]
        src_loaded = [sem(f"src_loaded{i}") for i in range(3)]
        gathered = [sem(f"gathered{i}") for i in range(3)]
        er_loaded = [sem(f"er_loaded{i}") for i in range(2)]

        def rows(ap, c, base):
            _, p, r = CH[min(base, NCH - 1)]
            r0 = c * (P * R) if base < FULL else CH[base][0]
            return ap[ds(r0, p * r), :].rearrange("(p r) d -> p (r d)", p=p), p, r * D

        def unit_slot(odd):
            return 1 if odd else 2

        def unit_count(half, odd):
            return half + (EARLY // 2 + 1 if odd else 1)

        block = ctx.enter_context(nc.Block())

        @block.sync
        def _(sp):
            def load_src(u, slot):
                sp.dma_start(src_slot[slot][:, :], src_main[:, ds(u * UT, UT)]).then_inc(src_loaded[slot], 16)

            def load_er(u, slot):
                sp.dma_start(er[slot][:, 0:UT * NB], er_main[:, ds(u * UT * NB, UT * NB)])\
                  .then_inc(er_loaded[slot], 16)

            def load_x(c, base):
                if base >= XS:
                    sp.wait_ge(s["o_done"], c - XS + 1)
                v, p, n = rows(x, c, base)
                sp.dma_start(xin[0:p, base % XS, 0:n], v).then_inc(x_loaded[base % XS], 16)

            def store(c, base):
                sp.wait_ge(s["o_done"], c + 1)
                v, p, n = rows(out, c, base)
                sp.dma_start(v, oc[0:p, base % XS, 0:n]).then_inc(stored[base % XS], 16)

            lt = T - NU * UT
            for c in range(2):
                load_x(c, c)
            sp.wait_ge(s["selfw_zero"], 1)
            sp.dma_start(wself32[0:MUL, 0:MUL], Ws).then_inc(s["selfw_loaded"], 16)
            for i in range(3):
                with nc.allow_non_contiguous_dma(reason="64 weights"):
                    sp.dma_start(wself32[MUL + i:D:3, MUL + i:D:3], Wv).then_inc(s["selfw_loaded"], 16)
            load_src(0, 0)
            for c in range(2, 4):
                load_x(c, c)
            load_src(1, 1)
            sp.wait_ge(s["selfw_scaled"], 1)
            for g in range(4):
                sp.dma_start(wself[g * D:(g + 1) * D, g * D:(g + 1) * D], wself32[:, :]).then_inc(s["selfw_placed"], 16)
            sp.wait_ge(s["zeroed"], 1)
            for k in range(4):
                sp.wait_ge(s["xT_ready"], k + 1)
                load_x(k + 4, k + 4)
                if k == 0:
                    for h in range(2):
                        sp.dma_start(b3f[:, h * NTP:(h + 1) * NTP], b3.rearrange("(a n) -> a n", a=1)).then_inc(s["w_loaded"], 16)
                        sp.dma_start(w3blk[h * HR:(h + 1) * HR, h * NTP:(h + 1) * NTP], W3).then_inc(s["w_loaded"], 16)
                if k == 1:
                    for h in range(2):
                        sp.dma_start(w2blk[h * HR:(h + 1) * HR, h * HR:(h + 1) * HR], W2).then_inc(s["w_loaded"], 16)
                        sp.dma_start(b1col[h * HR:(h + 1) * HR, :], b1.rearrange("(n a) -> n a", a=1)).then_inc(s["w_loaded"], 16)
                        sp.dma_start(b2col[h * HR:(h + 1) * HR, :], b2.rearrange("(n a) -> n a", a=1)).then_inc(s["w_loaded"], 16)
                if k == 2:
                    sp.dma_start(dst_i[:, 0:T], dst_main).then_inc(s["dst_loaded"], 16)
                    sp.dma_start(sh_all[:, 0:T * 4], sh_main).then_inc(s["sh_loaded"], 16)
                for t in (2 * k, 2 * k + 1):
                    sp.dma_start(w1big[t * NB:(t + 1) * NB, t // 2, (t % 2) * HR:(t % 2 + 1) * HR], W1)\
                      .then_inc(s["w_loaded"], 16)
            load_src(EARLY + 1, 2)
            load_er(0, 0)
            load_er(1, 1)
            sp.dma_start(er[2][:, 0:lt * NB], er_main[:, NU * UT * NB:T * NB]).then_inc(s["erlast_loaded"], 16)
            sp.dma_start(er[2][0:TAIL, lt * NB:(lt + 1) * NB], edge_radial[T * P:E, :]).then_inc(s["erlast_loaded"], 16)
            sp.dma_start(sh_all[0:TAIL, T * 4:T * 4 + 4], edge_sh[T * P:E, :]).then_inc(s["sh_loaded"], 16)
            sp.wait_ge(s["dst_pad"], 1)
            sp.dma_start(dst_i[0:TAIL, T:T + 1], dst[T * P:E].rearrange("(n a) -> n a", a=1)).then_inc(s["dst_loaded"], 16)
            sp.dma_start(out[N:N + BT * P, :].rearrange("(p r) d -> p (r d)", p=P), spare0[:, :]).then_inc(s["spare_stored"], 16)

            def node_pass(i, first):
                for k in range(DBODY):
                    c = i * DBODY + k
                    base = k if first else k + DBODY
                    if base >= XS:
                        store(c - XS, base - XS)
                        load_x(c, base)
                    if k in (3, 7):
                        slot = k // 4
                        sp.wait_ge(gathered[slot], (i + 1) * 16 * UT)
                        load_src(2 * i + 2 + slot, slot)

            node_pass(0, True)
            with sp.Fori(1, DLOOP - 1) as i:
                node_pass(i, False)
            for k in range(DBODY):
                c = (DLOOP - 1) * DBODY + k
                store(c - XS, c - XS)
                load_x(c, c)
                if k == 3:
                    sp.wait_ge(gathered[0], (EARLY // 2) * 16 * UT)
                    load_src(EARLY, 0)
            for c in range(FULL, NCH):
                store(c - XS, c - XS)
                load_x(c, c)
            for c in range(NCH - XS, NCH):
                store(c, c)

            def edge_pass(v, half, odd, tiles):
                for h in range(2):
                    sp.wait_ge(s["erT_ready"], 2 * v + h + 1)
                    load_er(2 * v + 2 + h, h)
                slot = unit_slot(odd)
                if tiles:
                    sp.wait_ge(gathered[slot], unit_count(half, odd) * 16 * UT)
                if tiles == UT:
                    load_src(EARLY + 3 + v, slot)
                elif tiles:
                    sp.dma_start(src_slot[slot][:, 0:lt], src_main[:, NU * UT:T]).then_inc(src_loaded[slot], 16)
                    sp.dma_start(src_slot[slot][0:TAIL, lt:lt + 1], src[T * P:E].rearrange("(n a) -> n a", a=1))\
                      .then_inc(src_loaded[slot], 16)

            sp.wait_ge(gathered[1], (EARLY // 2) * 16 * UT)
            load_src(EARLY + 2, 1)
            edge_pass(0, 0, 0, UT)
            with sp.Fori(0, HL - 1) as i:
                edge_pass(2 * i + 1, i, 1, UT)
                edge_pass(2 * i + 2, i + 1, 0, UT)
            v = NU // 2 - 3
            edge_pass(v, v // 2, 1, BT)
            edge_pass(v + 1, (v + 1) // 2, 0, 0)

        @block.gpsimd
        def _(pool):
            pool.memset(ident[:, :], 0.0).then_inc(s["pool_const"], 1)
            pool.wait_ge(s["pool_const"], 1)
            pool.affine_select(out=ident[:, :], in_=ident[:, :], compare_op=ALU.not_equal, fill=1.0, base=0,
                               pattern=[[-1, P]], channel_multiplier=1).then_inc(s["pool_const"], 1)

            def gather(t, slot):
                pool.indirect_dma_start(xg[slot][:, t * D:(t + 1) * D], None, x,
                                        bass.IndirectOffsetOnAxis(ap=src_slot[slot][:, t:t + 1], axis=0))\
                    .then_inc(gathered[slot], 16)

            def gather_early(i, first):
                for slot in range(2):
                    pool.wait_ge(src_loaded[slot], 16 * (i + 1))
                    if not first:
                        pool.wait_ge(s["gc_done"], 2 * i + slot - 1)
                        pool.nop(nofuse=True)
                    for t in range(UT):
                        gather(t, slot)

            gather_early(0, True)
            pool.iota(rank_w[:, :], pattern=[[1, 1]], base=(127 + 63) << 23, channel_multiplier=-(1 << 23))\
                .then_inc(s["pool_const"], 1)
            pool.iota(trash_i[:, :], pattern=[[P, BT]], base=N, channel_multiplier=1).then_inc(s["pool_const"], 1)
            pool.iota(dst_i[:, T:T + 1], pattern=[[1, 1]], base=N + (BT - 1) * P, channel_multiplier=1)\
                .then_inc(s["dst_pad"], 1)
            with pool.Fori(1, EARLY // 2) as i:
                gather_early(i, False)
            pool.wait_ge(src_loaded[0], 16 * (EARLY // 2 + 1))
            pool.wait_ge(s["gc_done"], EARLY - 1)
            for t in range(UT):
                gather(t, 0)
            pool.wait_ge(src_loaded[2], 16)
            for t in range(UT):
                gather(t, 2)

            def scatter(q, k):
                pool.wait_ge(s["idx_done"], q + 1)
                if k != 0:
                    pool.wait_ge(s["scattered"], q * 16 * BT)
                pool.nop(nofuse=True).then_inc(s["landed"], 1)
                for a in range(BT):
                    pool.indirect_dma_start(out, bass.IndirectOffsetOnAxis(ap=idx_i[:, k % NS, a:a + 1], axis=0),
                                            sums[:, k % NS, a * DR:a * DR + D], None, compute_op=ALU.add)\
                        .then_inc(s["scattered"], 16)

            def edge_pass(v, half, odd, first, tiles):
                slot, nodd = unit_slot(1 - odd), 1 - odd
                if tiles:
                    pool.wait_ge(src_loaded[slot], 16 * unit_count(half + odd, nodd) + (16 if tiles < UT else 0))
                    pool.wait_ge(s["gc_done"], EARLY + v + 1)
                    pool.nop(nofuse=True)
                for k in range(4):
                    for t in (2 * k, 2 * k + 1):
                        if t < tiles:
                            gather(t, slot)
                    scatter(4 * v + k, k if first else k + 4)

            for k in range(XS):
                pool.wait_ge(stored[k], 16 * len(range(k, NCH, XS)))
            pool.wait_ge(s["spare_stored"], 16)
            edge_pass(0, 0, 0, True, UT)
            with pool.Fori(0, HL - 1) as i:
                edge_pass(2 * i + 1, i, 1, False, UT)
                edge_pass(2 * i + 2, i + 1, 0, False, UT)
            for v in range(NU // 2 - 3, NU // 2):
                edge_pass(v, v // 2, v % 2, False, (UT, BT, 0)[v - NU // 2 + 3])
            scatter(NQ - 1, NQ - 1)
            pool.wait_ge(s["scattered"], NQ * 16 * BT)

        @block.scalar
        def _(act):
            def copy_xT(c, base):
                _, p, r = CH[base]
                n = r // 4 * P if base >= FULL else R * D
                act.wait_ge(s["xT_ready"], c + 1)
                if base >= 4:
                    act.wait_ge(s["xc_ready"], c - 3)
                act.activation(xTs[:, base // 2 % 2, 0:n], psXT[0][:, 0:n], ACT.Copy).then_inc(s["xT_copied"], 2)

            def relu_square(c, base):
                _, p, r = CH[base]
                n = r // 4 * P if base >= FULL else R * D
                if base % 2 == 0:
                    act.wait_ge(s["xc_ready"], c + 1)
                    centred = psXC[base // 2 % 2]
                else:
                    act.wait_ge(s["xT_ready"], c + 1)
                    centred = psXT[1]
                if base >= 2:
                    act.wait_ge(s["y_ready"], c - 1)
                if p < P:
                    n = p
                act.activation(sqT[:, base % 2, 0:n], centred[:, 0:n], ACT.Square)
                act.activation(rT[:, base % 2, 0:n], centred[:, 0:n], ACT.Relu).then_inc(s["rs_done"], 1)

            def node_std(c, base):
                _, p, r = CH[base]
                act.wait_ge(s["v_ready"], c + 1)
                if base >= 2:
                    act.wait_ge(s["rstd_done"], c - 1)
                act.activation(nstd[0:p, base % 2, 0:r], psV[base % 2][0:p, 0:r], ACT.Sqrt,
                               bias=epscol[0:p, :]).then_inc(s["std_done"], 1)

            def feat_square(n, w=UT * D):
                act.wait_ge(s["gc_done"], n + 1)
                act.activation(gsq[:, 0:w], gc[:, 0:w], ACT.Square).then_inc(s["gsq_done"], 1)

            def feat_std(n, w=UT):
                act.wait_ge(s["gvar_done"], n + 1)
                act.activation(gstd[:, 0:w], gvar[:, 0:w], ACT.Sqrt, bias=epscol[:, :], scale=1.0 / D)\
                   .then_inc(s["gstd_done"], 1)

            act.wait_ge(s["dve_const"], 1)
            act.activation(table_warm[:, :], epscol[:, :], ACT.Sqrt)

            def mlp_in(u, k):
                act.wait_ge(s["erT_ready"], u + 1)
                if k > 0:
                    act.wait_ge(s["l1_ready"], u)
                act.activation(erT[:, :], psER if k > 0 else psMLP[:, 0:P], ACT.Copy).then_inc(s["erT_copied"], 1)

            def mlp_one(u, k, w=4 * P):
                act.wait_ge(s["l1_ready"], u + 1)
                if k > 0:
                    act.wait_ge(s["l2_ready"], u)
                act.activation(x1[:, 0:w], psMLP[:, 0:w], ACT.Silu, bias=b1col[:, :]).then_inc(s["x1_done"], 1)

            def mlp_two(u, k, w=4 * P):
                act.wait_ge(s["l2_ready"], u + 1)
                if k > 1:
                    act.wait_ge(s["tp_ready"], 2 * u - 2)
                act.activation(x2[:, k % 2, 0:w], psMLP[:, 0:w], ACT.Silu, bias=b2col[:, :]).then_inc(s["x2_done"], 1)

            def dst_col(q, k):
                if k >= NS:
                    act.wait_ge(s["sq_done"], q - NS + 1)
                act.activation(dcol[:, k % NS, :], dst_f[:, ds(q * BT, BT)], ACT.Copy).then_inc(s["dcol_done"], 1)

            def node_step(c, base, i):
                if base < NCH and base % 2 == 0:
                    copy_xT(c, base)
                if 1 <= base <= NCH:
                    relu_square(c - 1, base - 1)
                if 2 <= base <= NCH + 1:
                    node_std(c - 2, base - 2)
                if 4 <= base < FULL:
                    n = 2 * i + base % 8 // 4 - 1
                    if base % 4 == 1:
                        feat_square(n)
                    if base % 4 == 3:
                        feat_std(n)
                if base in (FULL, FULL + 2):
                    feat_square(EARLY - 1 + (base - FULL) // 2)
                if base == FULL + 1:
                    feat_std(EARLY - 1)
                if base == 6:
                    mlp_in(0, 0)
                if base == FULL:
                    act.wait_ge(s["dst_cast"], 1)
                    for q in range(3):
                        dst_col(q, q)

            for k in range(DBODY):
                node_step(k, k, 0)
                if k == 7:
                    act.wait_ge(s["b3_split"], 1)
                    act.dma_start(b3rows[1:2, :], b3mid[:, :]).then_inc(s["b3_placed"], 16)
                    act.dma_start(b3rows[2:3, :], b3lo[:, :]).then_inc(s["b3_placed"], 16)
            with act.Fori(1, DLOOP) as i:
                for k in range(DBODY):
                    node_step(i * DBODY + k, k + DBODY, i)
            for c in range(FULL, NCH + 2):
                node_step(c, c, DLOOP)

            def copy_sums(q, k):
                act.wait_ge(s["sum_ready"], q + 1)
                if k >= NS:
                    act.wait_ge(s["landed"], q - NS + 2)
                act.activation(sums[:, k % NS, :], psSUM, ACT.Copy).then_inc(s["sums_done"], 1)

            def dst_square(q, k):
                act.wait_ge(s["dT_ready"], q + 1)
                act.wait_ge(s["dcol_done"], q + 1)
                if k >= 1:
                    act.wait_ge(s["eq_done"], q)
                for b in range(BT):
                    m = act.activation(dsq[:, b * BW:b * BW + (BT - b) * P], psDT[:, b * P:BW], ACT.Square,
                                       bias=dcol[:, k % NS, b:b + 1], scale=-1.0)
                m.then_inc(s["sq_done"], 1)

            def dst_equal(q, k):
                act.wait_ge(s["sq_done"], q + 1)
                if k >= 2:
                    act.wait_ge(s["sum_ready"], q - 1)
                if k >= NS:
                    act.wait_ge(s["idx_done"], q - NS + 1)
                e = eq[:, k % 2, :]
                act.activation(e.rearrange("p (b n) -> p b n", b=BT)[:, :, 0:P],
                               dsq[:, :].rearrange("p (b n) -> p b n", b=BT)[:, :, 0:P], ACT.Relu,
                               bias=onecol[:, :], scale=-4.0)
                for b in range(BT - 1):
                    o = slice(b * BW + P, b * BW + (BT - b) * P)
                    m = act.activation(e[:, o], dsq[:, o], ACT.Relu, bias=onecol[:, :], scale=-4.0,
                                       accum_out=lcnt[:, k % NS, b:b + 1])
                m.then_inc(s["eq_done"], 1)

            feat_std(EARLY)
            act.wait_ge(s["w_loaded"], 16 * (2 + 8 + UT))
            mlp_one(0, 0)
            mlp_in(1, 1)
            mlp_two(0, 0)
            dst_square(0, 0)
            mlp_one(1, 1)
            dst_equal(0, 0)
            mlp_two(1, 1)

            def edge_pass(v, first, last):
                n = EARLY + 1 + v
                for h in range(2):
                    u, k = 2 * v + h, (h if first else h + 4)
                    q, kq = 2 * u, 2 * k
                    end = last and h == 1
                    if not end:
                        mlp_in(u + 2, k + 2)
                    if not (first and h == 0):
                        copy_sums(q - 1, kq - 1)
                    dst_square(q + 1, kq + 1)
                    if h == 0 and not first:
                        feat_std(n - 1)
                    if not end:
                        mlp_one(u + 2, k + 2, 2 * P if last else 4 * P)
                        dst_col(q + 3, kq + 3)
                    dst_equal(q + 1, kq + 1)
                    if h == 1:
                        feat_square(n, BT * D if last else UT * D)
                    copy_sums(q, kq)
                    dst_square(q + 2, kq + 2)
                    if not end:
                        mlp_two(u + 2, k + 2, 2 * P if last else 4 * P)
                        dst_col(q + 4, kq + 4)
                    dst_equal(q + 2, kq + 2)

            edge_pass(0, True, False)
            with act.Fori(1, NU // 2 - 1) as v:
                edge_pass(v, False, False)
            edge_pass(NU // 2 - 1, False, True)
            feat_std(NU, BT)
            copy_sums(NQ - 2, NQ - 2)
            copy_sums(NQ - 1, NQ - 1)

        @block.tensor
        def _(pe):
            loop = {}

            def transposes(c, base):
                _, p, r = CH[base]
                if base % 2 == 0:
                    pe.wait_ge(x_loaded[base % XS], loaded_count(c, base))
                    rows_in = xin[0:p, base % XS, :]
                    if base >= 2:
                        pe.wait_ge(s["xT_copied"], c - 1)
                else:
                    pe.wait_ge(s["xc_done"], c + 1)
                    rows_in = xc[0:p, base // 2 % 2, :]
                    if base >= 2:
                        pe.wait_ge(s["rs_done"], c - 1)
                for g in range(r // 4):
                    m = pe.transpose(psXT[base % 2][:, g * P:g * P + p], rows_in[:, g * P:(g + 1) * P],
                                     ident[0:p, 0:p])
                m.then_inc(s["xT_ready"], 1)

            def loaded_count(c, base):
                if isinstance(c, int):
                    return 16 * (c // XS + 1)
                return loop["i"] * (16 * DBODY // XS) + 16 * ((base - DBODY) // XS + 1)

            def centre(c, base):
                _, p, r = CH[base]
                pe.wait_ge(s["xT_copied"], c + 1)
                if base >= 4:
                    pe.wait_ge(s["rs_done"], c - 3)
                n = r // 4 * P
                pe.matmul(psXC[base // 2 % 2][:, 0:n], center[:, :], xTs[:, base // 2 % 2, 0:n], start=True, stop=True)\
                  .then_inc(s["xc_ready"], 2)

            def products(c, base):
                _, p, r = CH[base]
                pe.wait_ge(s["rs_done"], c + 1)
                if base >= 1:
                    pe.wait_ge(s["std_done"], c)
                if base >= 2:
                    pe.wait_ge(s["y_used"], c - 1)
                for g in range(r // 4):
                    m = pe.matmul(psV[base % 2][0:p, 4 * g:4 * g + 4], sqT[:, base % 2, g * P:g * P + p], ones_g[:, :],
                                  start=True, stop=True)
                m.then_inc(s["v_ready"], 1)
                for g in range(r // 4):
                    m = pe.matmul(psY[base % 2][0:p, g * P:(g + 1) * P], rT[:, base % 2, g * P:g * P + p], wself[:, :],
                                  start=True, stop=True)
                m.then_inc(s["y_ready"], 1)

            def er_turn(u, k, slot, loads):
                if slot < 2:
                    pe.wait_ge(er_loaded[slot], 16 * loads)
                else:
                    pe.wait_ge(s["erlast_loaded"], 32)
                if k > 0:
                    pe.wait_ge(s["erT_copied"], u)
                if k == 0:
                    pe.transpose(psMLP[:, 0:P], er[slot][:, :], ident[:, :]).then_inc(s["erT_ready"], 1)
                    return
                if k == 1:
                    pe.wait_ge(s["std_done"], NCH)
                pe.transpose(psER, er[slot][:, :], ident[:, :]).then_inc(s["erT_ready"], 1)

            def layer1(u, k, pairs=4):
                pe.wait_ge(s["erT_copied"], u + 1)
                if k > 0:
                    pe.wait_ge(s["x2_done"], u)
                for j in range(pairs):
                    m = pe.matmul(psMLP[:, j * P:(j + 1) * P], w1big[:, j, :], erT[:, :], start=True, stop=True)
                m.then_inc(s["l1_ready"], 1)

            def layer2(u, k, pairs=4):
                pe.wait_ge(s["x1_done"], u + 1)
                pe.matmul(psMLP[:, 0:pairs * P], w2blk[:, :], x1[:, 0:pairs * P], start=True, stop=True)\
                  .then_inc(s["l2_ready"], 1)

            def layer3(q, k, u):
                pe.wait_ge(s["x2_done"], u + 1)
                if k >= 2:
                    pe.wait_ge(s["prod_done"], q - 1)
                else:
                    pe.wait_ge(s["rs_done"], NCH)
                    pe.wait_ge(s["xT_copied"], NCH)
                for h in range(2):
                    j = 2 * (k % 2) + h
                    o = psTP[k % 2][:, h * 2 * NTP:(h + 1) * 2 * NTP]
                    pe.matmul(o, x2[:, k // 2 % 2, j * P:(j + 1) * P], w3blk[:, :], start=True, stop=False)
                    m = pe.matmul(o, ones3[:, :], b3rows[:, :], start=False, stop=True)
                m.then_inc(s["tp_ready"], 1)

            def dst_rows(q, k):
                pe.wait_ge(s["dcol_done"], q + 1)
                if k >= 1:
                    pe.wait_ge(s["sq_done"], q)
                else:
                    pe.wait_ge(s["y_used"], NCH - 1)
                for b in range(BT):
                    m = pe.transpose(psDT[:, b * P:(b + 1) * P], dcol[:, k % NS, b:b + 1].to_broadcast([P, P]), ident[:, :])
                m.then_inc(s["dT_ready"], 1)

            def node_step(c, base):
                if base < NCH:
                    transposes(c, base)
                if 1 <= base <= NCH and base % 2 == 1:
                    centre(c - 1, base - 1)
                if 2 <= base <= NCH + 1:
                    if base == 2:
                        pe.wait_ge(s["selfw_placed"], 64)
                    products(c - 2, base - 2)
                if base == 6:
                    er_turn(0, 0, 0, 1)
                if base == 7:
                    pe.wait_ge(s["w_loaded"], 16 * (2 + 8 + UT))
                    layer1(0, 0)

            pe.wait_ge(s["pool_const"], 2)
            pe.wait_ge(s["dve_const"], 2)
            for k in range(DBODY):
                node_step(k, k)
            with pe.Fori(1, DLOOP) as i:
                loop["i"] = i
                for k in range(DBODY):
                    node_step(i * DBODY + k, k + DBODY)
            for c in range(FULL, NCH + 2):
                node_step(c, c)

            def sum_batch(q, k):
                pe.wait_ge(s["msg_done"], q + 1)
                pe.wait_ge(s["eq_done"], q + 1)
                if k >= 1:
                    pe.wait_ge(s["sums_done"], q)
                for a in range(BT):
                    for b in [a] + list(range(a)):
                        o, n = b * BW + (a - b) * P, (DR if b == a else D)
                        m = pe.matmul(psSUM[:, a * DR:a * DR + n], eq[:, k % 2, o:o + P], msg[:, k % 2, b, 0:n],
                                      start=(b == a), stop=(b == a - 1 or a == 0))
                m.then_inc(s["sum_ready"], 1)

            er_turn(1, 1, 1, 1)
            layer2(0, 0)
            dst_rows(0, 0)
            pe.wait_ge(s["b3_placed"], 32)
            layer3(0, 0, 0)
            layer1(1, 1)
            layer2(1, 1)

            def edge_pass(v, first, last):
                for h in range(2):
                    u, k = 2 * v + h, (h if first else h + 4)
                    q, kq = 2 * u, 2 * k
                    end = last and h == 1
                    layer3(q + 1, kq + 1, u)
                    dst_rows(q + 1, kq + 1)
                    if not end:
                        er_turn(u + 2, k + 2, 2 if last else h, v + 2)
                    if not (first and h == 0):
                        sum_batch(q - 1, kq - 1)
                    if not end:
                        layer1(u + 2, k + 2, 2 if last else 4)
                    layer3(q + 2, kq + 2, u + 1)
                    dst_rows(q + 2, kq + 2)
                    sum_batch(q, kq)
                    if not end:
                        layer2(u + 2, k + 2, 2 if last else 4)

            edge_pass(0, True, False)
            with pe.Fori(1, NU // 2 - 1) as v:
                edge_pass(v, False, False)
            edge_pass(NU // 2 - 1, False, True)
            sum_batch(NQ - 2, NQ - 2)
            sum_batch(NQ - 1, NQ - 1)

        @block.vector
        def _(dve):
            dve.memset(onecol[:, :], 1.0)
            dve.memset(epscol[:, :], EPS).then_inc(s["dve_const"], 1)
            dve.memset(wself32[:, :], 0.0)
            dve.memset(wself[:, :], 0.0).then_inc(s["selfw_zero"], 1)
            for t in (er[0], er[1], er[2], w2blk, w3blk):
                dve.memset(t[:, :], 0.0)
            dve.memset(w1big[:, :, :], 0.0)
            dve.memset(lcnt[:, :, :], 0.0)
            dve.memset(sh_all[:, T * 4:T * 4 + 4], 0.0)
            dve.memset(spare0[:, :], 0.0)
            dve.memset(b3rows[:, :], 0.0).then_inc(s["zeroed"], 1)
            dve.memset(ones_g[:, :], 0.0)
            dve.memset(center[:, :], 0.0)
            dve.memset(ones3[:, :], 0.0).then_inc(s["dve_zero"], 1)
            dve.wait_ge(s["dve_zero"], 1)
            dve.memset(ones3[0:3, :], 1.0)
            for g in range(4):
                dve.memset(ones_g[g * D:(g + 1) * D, g:g + 1], 1.0 / D)
                m = dve.memset(center[g * D:(g + 1) * D, g * D:(g + 1) * D], -1.0 / D)
            m.then_inc(s["dve_zero"], 1)
            dve.wait_ge(s["dve_zero"], 2)
            dve.wait_ge(s["pool_const"], 2)
            dve.tensor_tensor(center[:, :], center[:, :], ident[:, :], ALU.add).then_inc(s["dve_const"], 1)

            def scale_weights():
                dve.wait_ge(s["w_loaded"], 16 * (2 + 8 + UT))
                for w in (w3blk, b3f):
                    v = w[:, :].rearrange("p (h n) -> p h n", h=2)
                    dve.tensor_scalar(v[:, :, 0:MUL * MUL], v[:, :, 0:MUL * MUL], SCALE, None, ALU.mult)
                    dve.tensor_scalar(v[:, :, 2 * MUL * MUL:NTP], v[:, :, 2 * MUL * MUL:NTP], SCALE, None, ALU.mult)
                    m = dve.tensor_scalar(v[:, :, MUL * MUL:2 * MUL * MUL], v[:, :, MUL * MUL:2 * MUL * MUL],
                                          SCALE * INV_SQRT3, None, ALU.mult)
                    m.then_inc(s["b3_scaled"], 1)
                dve.wait_ge(s["b3_scaled"], 2)
                dve.tensor_copy(b3rows[0:1, :], b3f[:, :]).then_inc(s["b3_scaled"], 1)
                dve.wait_ge(s["b3_scaled"], 3)
                dve.tensor_tensor(b3f[:, :], b3f[:, :], b3rows[0:1, :], ALU.subtract).then_inc(s["b3_scaled"], 1)
                dve.wait_ge(s["b3_scaled"], 4)
                dve.tensor_copy(b3mid[:, :], b3f[:, :]).then_inc(s["b3_scaled"], 1)
                dve.wait_ge(s["b3_scaled"], 5)
                dve.tensor_tensor(b3r[:, :], b3f[:, :], b3mid[:, :], ALU.subtract).then_inc(s["b3_scaled"], 1)
                dve.wait_ge(s["b3_scaled"], 6)
                dve.tensor_copy(b3lo[:, :], b3r[:, :]).then_inc(s["b3_split"], 1)

            def row_sums(c, base):
                _, p, r = CH[base]
                dve.wait_ge(x_loaded[base % XS], loaded_count(c, base))
                dve.tensor_reduce(nsum[0:p, base // 2 % 2, 0:r], xin[0:p, base % XS, 0:r * D].rearrange("p (r d) -> p r d", d=D),
                                  X, ALU.add).then_inc(s["xsum_done"], 2)

            def centre_rows(c, base):
                _, p, r = CH[base]
                k = base // 2 % 2
                if base >= 4:
                    dve.wait_ge(s["xT_ready"], c - 3)
                dve.wait_ge(s["xsum_done"], c + 1)
                dve.scalar_tensor_tensor(out=xc[0:p, k, 0:r * D].rearrange("p (r d) -> p r d", d=D),
                                         in0=nsum[0:p, k, 0:r].rearrange("p (r a) -> p r a", a=1).to_broadcast([p, r, D]),
                                         scalar=-1.0 / D, in1=xin[0:p, base % XS, 0:r * D].rearrange("p (r d) -> p r d", d=D),
                                         op0=ALU.mult, op1=ALU.add).then_inc(s["xc_done"], 2)

            def loaded_count(c, base):
                if isinstance(c, int):
                    return 16 * (c // XS + 1)
                return loop["i"] * (16 * DBODY // XS) + 16 * ((base - DBODY) // XS + 1)

            def node_rstd(c, base):
                _, p, r = CH[base]
                dve.wait_ge(s["std_done"], c + 1)
                dve.reciprocal(nrstd[0:p, base % 2, 0:r], nstd[0:p, base % 2, 0:r]).then_inc(s["rstd_done"], 1)

            def node_scale(c, base):
                _, p, r = CH[base]
                dve.wait_ge(s["y_ready"], c + 1)
                dve.wait_ge(s["rstd_done"], c + 1)
                if base >= XS:
                    dve.wait_ge(stored[base % XS], store_count(c, base))
                o = oc[0:p, base % XS, 0:r * D].rearrange("p (r d) -> p r d", d=D)
                dve.tensor_tensor(o, psY[base % 2][0:p, 0:r * D].rearrange("p (r d) -> p r d", d=D),
                                  nrstd[0:p, base % 2, 0:r].rearrange("p (r a) -> p r a", a=1).to_broadcast([p, r, D]),
                                  ALU.mult).then_inc(s["y_used"], 1)

            def node_add(c, base):
                _, p, r = CH[base]
                dve.wait_ge(s["y_used"], c + 1)
                dve.tensor_tensor(oc[0:p, base % XS, 0:r * D], oc[0:p, base % XS, 0:r * D], xin[0:p, base % XS, 0:r * D],
                                  ALU.add).then_inc(s["o_done"], 1)

            loop = {}

            def store_count(c, base):
                if isinstance(c, int):
                    return 16 * (c // XS)
                return loop["i"] * (16 * DBODY // XS) + 16 * ((base - DBODY) // XS)

            def gathered_rows(slot, w):
                return xg[slot][:, 0:w * D].rearrange("p (t d) -> p t d", d=D)

            def feat_sum(n, slot, count, w=UT):
                dve.wait_ge(gathered[slot], count)
                dve.tensor_reduce(gsum[:, 0:w], gathered_rows(slot, w), X, ALU.add).then_inc(s["gsum_done"], 1)

            def feat_centre(n, slot, w=UT):
                dve.wait_ge(s["gsum_done"], n + 1)
                if not isinstance(n, int) or n > 0:
                    dve.wait_ge(s["h_done"], n)
                dve.scalar_tensor_tensor(out=gc[:, 0:w * D].rearrange("p (t d) -> p t d", d=D),
                                         in0=gsum[:, 0:w].rearrange("p (t a) -> p t a", a=1).to_broadcast([P, w, D]),
                                         scalar=-1.0 / D, in1=gathered_rows(slot, w), op0=ALU.mult, op1=ALU.add)\
                   .then_inc(s["gc_done"], 1)

            def feat_var(n, w=UT):
                dve.wait_ge(s["gsq_done"], n + 1)
                dve.tensor_reduce(gvar[:, 0:w], gsq[:, 0:w * D].rearrange("p (t d) -> p t d", d=D), X, ALU.add)\
                   .then_inc(s["gvar_done"], 1)

            def feat_rstd(n, w=UT):
                dve.wait_ge(s["gstd_done"], n + 1)
                dve.reciprocal(grstd[:, 0:w], gstd[:, 0:w]).then_inc(s["grstd_done"], 1)

            def feat_scale(n, w=UT):
                dve.wait_ge(s["grstd_done"], n + 1)
                dve.scalar_tensor_tensor(out=h_all[:, ds(n * (UT * D), w * D)].rearrange("p (t d) -> p t d", d=D),
                                         in0=gc[:, 0:w * D].rearrange("p (t d) -> p t d", d=D), scalar=0.0,
                                         in1=grstd[:, 0:w].rearrange("p (t a) -> p t a", a=1).to_broadcast([P, w, D]),
                                         op0=ALU.max, op1=ALU.mult).then_inc(s["h_done"], 1)

            def node_step(c, base, i):
                n = 2 * i + base % 8 // 4 - 1
                slot, count = (base // 4 - 1) % 2, (i + (1 if base % 8 // 4 else 0)) * (16 * UT)
                ahead = base % 2 == 1 and base + 2 < NCH
                out_too = 2 <= base <= NCH + 1
                centring = 4 <= base <= FULL and base % 4 == 0
                scaling = centring and base >= 8
                if base == FULL + 2:
                    n, slot, count, centring, scaling = EARLY, 0, (EARLY // 2 + 1) * (16 * UT), True, True
                if ahead:
                    row_sums(c + 2, base + 2)
                if base == FULL + 3:
                    feat_var(EARLY)
                if scaling:
                    feat_rstd(n - 1)
                if centring:
                    feat_sum(n, slot, count)
                if out_too:
                    node_rstd(c - 2, base - 2)
                if scaling:
                    feat_scale(n - 1)
                if base % 4 == 2 and 4 <= base < FULL:
                    feat_var(n)
                if base == FULL + 1:
                    feat_var(EARLY - 1)
                if ahead:
                    centre_rows(c + 2, base + 2)
                if out_too:
                    node_scale(c - 2, base - 2)
                if centring:
                    feat_centre(n, slot)
                if out_too:
                    node_add(c - 2, base - 2)

            row_sums(1, 1)
            centre_rows(1, 1)
            dve.wait_ge(s["selfw_loaded"], 64)
            dve.tensor_scalar(wself32[:, :], wself32[:, :], SELF, None, ALU.mult).then_inc(s["selfw_scaled"], 1)
            for k in range(DBODY):
                node_step(k, k, 0)
                if k == 6:
                    scale_weights()
            dve.wait_ge(s["pool_const"], 4)
            dve.tensor_copy(trash[:, :], trash_i[:, :])
            rw = rank_w[:, :].bitcast(f32)
            dve.tensor_scalar(rank_max[:, :], rw, 2.5, None, ALU.mult)
            for k in range(2):
                for b in range(BT):
                    dve.tensor_copy(msg[:, k, b, D:DR], rw)
            dve.wait_ge(s["dst_loaded"], 32)
            dve.tensor_copy(dst_f[:, :], dst_i[:, :]).then_inc(s["dst_cast"], 1)
            dve.wait_ge(s["dst_cast"], 1)
            dve.tensor_tensor(dmt_all[:, :].rearrange("p (q t) -> p q t", t=BT),
                              dst_f[:, :].rearrange("p (q t) -> p q t", t=BT),
                              trash[:, :].rearrange("p (a t) -> p a t", a=1).to_broadcast([P, NQ, BT]), ALU.subtract)
            with dve.Fori(1, DLOOP) as i:
                loop["i"] = i
                for k in range(DBODY):
                    node_step(i * DBODY + k, k + DBODY, i)
            for c in range(FULL, NCH + 2):
                node_step(c, c, DLOOP)

            def coefs(u, k, w=UT):
                t0 = u * UT
                hs = h_all[:, ds(t0 * D, w * D)].rearrange("p (t d) -> p t d", d=D)[:, :, 0:MUL]
                hv = h_all[:, ds(t0 * D, w * D)].rearrange("p (t d) -> p t d", d=D)[:, :, MUL:D]
                sh = sh_all[:, ds(t0 * 4, w * 4)].rearrange("p (t k) -> p t k", k=4)
                c = coef[:, k % 2, 0:w, :]
                dp = dotp[:, 0:w * 24].rearrange("p (t u i) -> p t u i", u=MUL, i=3)
                dve.tensor_tensor(dp, hv.rearrange("p t (u i) -> p t u i", i=3),
                                  sh[:, :, 1:4].rearrange("p t (a i) -> p t a i", a=1).to_broadcast([P, w, MUL, 3]),
                                  ALU.mult)
                m = dve.tensor_tensor(c[:, :, 0:MUL], hs, sh[:, :, 0:1].to_broadcast([P, w, MUL]), ALU.mult)
                m.then_inc(s["dot_done"], 1)
                dve.tensor_tensor(c[:, :, 3 * MUL:6 * MUL].rearrange("p t (i u) -> p t i u", i=3),
                                  hv.rearrange("p t (u i) -> p t i u", i=3),
                                  sh[:, :, 0:1].rearrange("p t (a i) -> p t a i", a=1).to_broadcast([P, w, 3, MUL]),
                                  ALU.mult)
                dve.tensor_copy(c[:, :, 2 * MUL:3 * MUL], hs)
                dve.wait_ge(s["dot_done"], u + 1)
                dve.tensor_reduce(c[:, :, MUL:2 * MUL], dp, X, ALU.add).then_inc(s["coef_done"], 1)

            def index_rank(q, k):
                dve.wait_ge(s["sums_done"], q + 1)
                rank = sums[:, k % NS, :].rearrange("p (t d) -> p t d", d=DR)[:, :, D]
                dve.scalar_tensor_tensor(out=first[:, :], in0=rank, scalar=rank_max[:, :], in1=dmt_all[:, ds(q * BT, BT)],
                                         op0=ALU.is_lt, op1=ALU.mult).then_inc(s["first_done"], 1)

            def index_later(q, k):
                dve.wait_ge(s["eq_done"], q + 1)
                dve.wait_ge(s["first_done"], q + 1)
                dve.scalar_tensor_tensor(out=idx_f[:, :], in0=lcnt[:, k % NS, :], scalar=0.5, in1=first[:, :],
                                         op0=ALU.is_lt, op1=ALU.mult).then_inc(s["idxf_done"], 1)

            def index_out(q, k):
                dve.wait_ge(s["idxf_done"], q + 1)
                dve.tensor_tensor(idx_i[:, k % NS, :], idx_f[:, :], trash[:, :], ALU.add).then_inc(s["idx_done"], 1)

            def products(q, k, u):
                r = k % 2
                w = psTP[k % 2].rearrange("p (t n) -> p t n", n=NTP)
                c = coef[:, k // 2 % 2, r * BT:(r + 1) * BT, :]
                dve.wait_ge(s["tp_ready"], q + 1)
                dve.wait_ge(s["coef_done"], u + 1)
                dve.tensor_tensor(prod[:, :, 0:192].rearrange("p t (g w) -> p t g w", w=MUL),
                                  w[:, :, 0:192].rearrange("p t (g w) -> p t g w", w=MUL),
                                  c[:, :, 0:24].rearrange("p t (g a) -> p t g a", a=1).to_broadcast([P, BT, 24, MUL]), ALU.mult)
                for i in range(3):
                    m = dve.tensor_tensor(prod[:, :, 192 + 64 * i:256 + 64 * i].rearrange("p t (g w) -> p t g w", w=MUL),
                                          w[:, :, 192:256].rearrange("p t (g w) -> p t g w", w=MUL),
                                          c[:, :, 24 + 8 * i:32 + 8 * i].rearrange("p t (g a) -> p t g a", a=1)
                                          .to_broadcast([P, BT, MUL, MUL]), ALU.mult)
                m.then_inc(s["prod_done"], 1)

            def sum_vectors(q, k):
                dve.wait_ge(s["prod_done"], q + 1)
                dve.tensor_reduce(red[:, :, :, :], prod[:, :, 128:384].rearrange("p t (g u w) -> p t g w u", u=MUL, w=MUL),
                                  X, ALU.add).then_inc(s["red_done"], 1)

            def sum_scalars(q, k):
                if k >= 2:
                    dve.wait_ge(s["sum_ready"], q - 1)
                dve.tensor_reduce(msg[:, k % 2, :, 0:MUL], prod[:, :, 0:128].rearrange("p t (u w) -> p t w u", w=MUL),
                                  X, ALU.add)

            def outer_product(q, k):
                dve.wait_ge(s["red_done"], q + 1)
                sh1 = sh_all[:, ds(q * (BT * 4), BT * 4)].rearrange("p (t k) -> p t k", k=4)[:, :, 1:4]
                dve.tensor_tensor(outer[:, :, :].rearrange("p t (w i) -> p t w i", i=3),
                                  red[:, :, 0, :].rearrange("p t (w a) -> p t w a", a=1).to_broadcast([P, BT, MUL, 3]),
                                  sh1.rearrange("p t (a i) -> p t a i", a=1).to_broadcast([P, BT, MUL, 3]), ALU.mult)\
                   .then_inc(s["outer_done"], 1)

            def vectors(q, k):
                dve.wait_ge(s["outer_done"], q + 1)
                dve.tensor_tensor(msg[:, k % 2, :, MUL:D].rearrange("p t (w i) -> p t w i", i=3),
                                  outer[:, :, :].rearrange("p t (w i) -> p t w i", i=3),
                                  red[:, :, 1:4, :].rearrange("p t i w -> p t w i"), ALU.add).then_inc(s["msg_done"], 1)

            dve.wait_ge(s["sh_loaded"], 32)

            def edge_pass(v, half, odd, first, last):
                n = EARLY + 1 + v
                fw = BT if last else UT
                slot = unit_slot(odd)
                count = unit_count(half, odd) * (16 * UT) - (16 * (UT - BT) if last else 0)
                for h in range(2):
                    u, ku = 2 * v + h, (h if first else h + 4)
                    dve.wait_ge(s["h_done"], n - 1 + h)
                    coefs(u, ku)
                    if first and h == 1:
                        index_rank(0, 0)
                        index_later(0, 0)
                        index_out(0, 0)
                    for r in range(2):
                        q, k = 2 * u + r, 2 * ku + r
                        ready = not first or h * r == 1
                        products(q, k, u)
                        if h == 1 and r == 0:
                            feat_sum(n, slot, count, fw)
                        if ready:
                            index_rank(q - 2, k - 2)
                        sum_vectors(q, k)
                        if h == 1 and r == 0:
                            feat_centre(n, slot, fw)
                        if ready:
                            index_later(q - 2, k - 2)
                        if h == 0 and r == 0 and not first:
                            feat_var(n - 1)
                        sum_scalars(q, k)
                        if ready:
                            index_out(q - 2, k - 2)
                        outer_product(q, k)
                        if h == 0 and r == 1:
                            feat_rstd(n - 1)
                        vectors(q, k)
                        if h == 0 and r == 1:
                            feat_scale(n - 1)

            edge_pass(0, 0, 0, True, False)
            with dve.Fori(0, HL) as i:
                edge_pass(2 * i + 1, i, 1, False, False)
                edge_pass(2 * i + 2, i + 1, 0, False, False)
            v = NU // 2 - 1
            edge_pass(v, v // 2, 1, False, True)
            feat_var(NU, BT)
            feat_rstd(NU, BT)
            feat_scale(NU, BT)
            q = NQ - 1
            dve.wait_ge(s["h_done"], NU + 1)
            coefs(NU, NU, BT)
            products(q, q, NU)
            index_rank(q - 2, q - 2)
            sum_vectors(q, q)
            index_later(q - 2, q - 2)
            sum_scalars(q, q)
            index_out(q - 2, q - 2)
            outer_product(q, q)
            vectors(q, q)
            index_rank(q - 1, q - 1)
            index_later(q - 1, q - 1)
            index_out(q - 1, q - 1)
            index_rank(q, q)
            index_later(q, q)
            index_out(q, q)


_INS = ["x", "src", "dst", "edge_attr_4", "edge_attr_8", "L0_gnn_W1", "L0_gnn_b1", "L0_gnn_W2", "L0_gnn_b2",
        "L0_gnn_W3", "L0_gnn_b3", "L0_gnn_Ws", "L0_gnn_Wv"]


def kernel(**inputs):
    import numpy as _np
    import concourse.bacc as _bacc
    from concourse import mybir as _mybir
    from concourse.bass_utils import run_bass_kernel_spmd as _run

    nc = _bacc.Bacc("TRN2", target_bir_lowering=False, num_devices=1)
    arrays, args = {}, []
    for name in _INS:
        a = _np.ascontiguousarray(inputs[name])
        arrays[f"in_{name}_dram"] = a
        args.append(nc.dram_tensor(f"in_{name}_dram", a.shape, _mybir.dt.from_np(a.dtype), kind="ExternalInput").ap())
    n, d = inputs["x"].shape
    spare = 4 * 128
    args.append(nc.dram_tensor("out_dram", (n + spare, d), _mybir.dt.float32, kind="ExternalOutput").ap())
    gnn_layer(nc, *args)
    r = _run(nc, [arrays], core_ids=[0])
    return r.results[0]["out_dram"][:n]
```
